# Optimizing a Trainium2 kernel written in Bass

```python
import numpy as np
import jax
import jax.numpy as jnp

def _softmax(x, axis=-1):
    return jax.nn.softmax(x, axis=axis)

def _gelu(x):
    return jax.nn.gelu(x, approximate=True)

def _silu(x):
    return jax.nn.silu(x)

def _sigmoid(x):
    return jax.nn.sigmoid(x)

def _layernorm(x, axis=-1, eps=1e-05):
    m = jnp.mean(x, axis=axis, keepdims=True)
    v = jnp.var(x, axis=axis, keepdims=True)
    return (x - m) / jnp.sqrt(v + eps)

def _scatter_add(tgt, idx, src, axis=0):
    return tgt.at[idx].add(src)

def _segment_sum(src, seg, n):
    return jax.ops.segment_sum(src, seg, n)
kernel_name = 'mk_seq_preln_d1_jaxref_r4_6e9f82'

def setup_inputs(seed: int=0):
    np.random.seed(seed)
    _w = jnp.asarray

    def _L0_attn_setup():
        import jax, jax.numpy as jnp
        import numpy as np
        D_MODEL = 256
        D_STATE = 16
        EXPAND = 2
        D_INNER = D_MODEL * EXPAND
        DT_RANK = D_MODEL // 16

        def _ssm_forward(u, W_in, b_in, W_x, b_x, W_dt, b_dt, A_log, D, W_out, b_out):
            B, T, _ = u.shape
            u_inner = u @ W_in.T + b_in
            x, z = jnp.split(u_inner, 2, axis=-1)
            dbc = x @ W_x.T + b_x
            delta_raw = dbc[..., :DT_RANK]
            B_ssm = dbc[..., DT_RANK:DT_RANK + D_STATE]
            C_ssm = dbc[..., DT_RANK + D_STATE:]
            delta = jax.nn.softplus(delta_raw @ W_dt.T + b_dt)
            A = -jnp.exp(A_log)

            def step(h, xs):
                dt_t, x_t, Bt, Ct = xs
                dA = jnp.exp(dt_t[..., None] * A)
                dB = dt_t[..., None] * Bt[:, None, :]
                h = h * dA + x_t[..., None] * dB
                y_t = jnp.einsum('bdn,bn->bd', h, Ct)
                return (h, y_t)
            h0 = jnp.zeros((B, D_INNER, D_STATE), u.dtype)
            xs = (jnp.swapaxes(delta, 0, 1), jnp.swapaxes(x, 0, 1), jnp.swapaxes(B_ssm, 0, 1), jnp.swapaxes(C_ssm, 0, 1))
            _, y = jax.lax.scan(step, h0, xs)
            y = jnp.swapaxes(y, 0, 1)
            y = y + x * D
            y = y * (z * jax.nn.sigmoid(z))
            return y @ W_out.T + b_out
        key = jax.random.key(seed)
        ks = jax.random.split(key, 12)
        B, T = (2, 512)
        s_in = 1.0 / np.sqrt(D_MODEL)
        s_x = 1.0 / np.sqrt(D_INNER)
        s_dt = 1.0 / np.sqrt(DT_RANK)
        inp = {'u': jax.random.normal(ks[0], (B, T, D_MODEL), jnp.float32), 'W_in': jax.random.uniform(ks[1], (2 * D_INNER, D_MODEL), jnp.float32, -s_in, s_in), 'b_in': jax.random.uniform(ks[2], (2 * D_INNER,), jnp.float32, -s_in, s_in), 'W_x': jax.random.uniform(ks[3], (DT_RANK + 2 * D_STATE, D_INNER), jnp.float32, -s_x, s_x), 'b_x': jax.random.uniform(ks[4], (DT_RANK + 2 * D_STATE,), jnp.float32, -s_x, s_x), 'W_dt': jax.random.uniform(ks[5], (D_INNER, DT_RANK), jnp.float32, -s_dt, s_dt), 'b_dt': jax.random.uniform(ks[6], (D_INNER,), jnp.float32, -s_dt, s_dt), 'A_log': jnp.log(jnp.abs(jax.random.normal(ks[7], (D_INNER, D_STATE), jnp.float32)) + 1e-06), 'D': jnp.ones((D_INNER,), jnp.float32), 'W_out': jax.random.uniform(ks[8], (D_MODEL, D_INNER), jnp.float32, -s_x, s_x), 'b_out': jax.random.uniform(ks[9], (D_MODEL,), jnp.float32, -s_x, s_x)}
        return inp
    _L0_attn_in = _L0_attn_setup()

    def _L0_ffn_setup():
        import jax, jax.numpy as jnp
        import numpy as np
        TOP_K = 2
        key = jax.random.key(seed)
        ks = jax.random.split(key, 7)
        B_, S, D, F, E, R = (2, 512, 256, 1024, 4, 4)
        x = jax.random.normal(ks[0], (B_, S, D), dtype=jnp.float32)
        Wg = jax.random.normal(ks[1], (E, D), dtype=jnp.float32) * (1.0 / np.sqrt(D))
        bg = jnp.zeros((E,), dtype=jnp.float32)
        Wi = jax.random.normal(ks[2], (F, D), dtype=jnp.float32) * (1.0 / np.sqrt(D))
        Wo = jax.random.normal(ks[3], (D, F), dtype=jnp.float32) * (1.0 / np.sqrt(F))
        A = jax.random.normal(ks[4], (E, R, D), dtype=jnp.float32) * (1.0 / np.sqrt(D))
        Bm = jax.random.normal(ks[5], (E, F, R), dtype=jnp.float32) * 0.01
        return {'x': x, 'Wg': Wg, 'bg': bg, 'Wi': Wi, 'Wo': Wo, 'A': A, 'B': Bm}
    _L0_ffn_in = _L0_ffn_setup()
    _d = {'L0_attn_u': _L0_attn_in['u'], 'L0_attn_W_in': _L0_attn_in['W_in'], 'L0_attn_b_in': _L0_attn_in['b_in'], 'L0_attn_W_x': _L0_attn_in['W_x'], 'L0_attn_b_x': _L0_attn_in['b_x'], 'L0_attn_W_dt': _L0_attn_in['W_dt'], 'L0_attn_b_dt': _L0_attn_in['b_dt'], 'L0_attn_A_log': _L0_attn_in['A_log'], 'L0_attn_D': _L0_attn_in['D'], 'L0_attn_W_out': _L0_attn_in['W_out'], 'L0_attn_b_out': _L0_attn_in['b_out'], 'L0_ffn_Wg': _L0_ffn_in['Wg'], 'L0_ffn_bg': _L0_ffn_in['bg'], 'L0_ffn_Wi': _L0_ffn_in['Wi'], 'L0_ffn_Wo': _L0_ffn_in['Wo'], 'L0_ffn_A': _L0_ffn_in['A'], 'L0_ffn_B': _L0_ffn_in['B']}
    _x0 = _d['L0_attn_u']
    _d['L0_attn_u'] = jax.random.normal(jax.random.fold_in(jax.random.key(seed), 1), (4, 2048, 256), dtype=_x0.dtype)
    del _x0
    return _d

def reference(L0_attn_u, L0_attn_W_in, L0_attn_b_in, L0_attn_W_x, L0_attn_b_x, L0_attn_W_dt, L0_attn_b_dt, L0_attn_A_log, L0_attn_D, L0_attn_W_out, L0_attn_b_out, L0_ffn_Wg, L0_ffn_bg, L0_ffn_Wi, L0_ffn_Wo, L0_ffn_A, L0_ffn_B):

    def _L0_attn_ref(u, W_in, b_in, W_x, b_x, W_dt, b_dt, A_log, D, W_out, b_out):
        import jax, jax.numpy as jnp
        import numpy as np
        D_MODEL = 256
        D_STATE = 16
        EXPAND = 2
        D_INNER = D_MODEL * EXPAND
        DT_RANK = D_MODEL // 16

        def _ssm_forward(u, W_in, b_in, W_x, b_x, W_dt, b_dt, A_log, D, W_out, b_out):
            B, T, _ = u.shape
            u_inner = u @ W_in.T + b_in
            x, z = jnp.split(u_inner, 2, axis=-1)
            dbc = x @ W_x.T + b_x
            delta_raw = dbc[..., :DT_RANK]
            B_ssm = dbc[..., DT_RANK:DT_RANK + D_STATE]
            C_ssm = dbc[..., DT_RANK + D_STATE:]
            delta = jax.nn.softplus(delta_raw @ W_dt.T + b_dt)
            A = -jnp.exp(A_log)

            def step(h, xs):
                dt_t, x_t, Bt, Ct = xs
                dA = jnp.exp(dt_t[..., None] * A)
                dB = dt_t[..., None] * Bt[:, None, :]
                h = h * dA + x_t[..., None] * dB
                y_t = jnp.einsum('bdn,bn->bd', h, Ct)
                return (h, y_t)
            h0 = jnp.zeros((B, D_INNER, D_STATE), u.dtype)
            xs = (jnp.swapaxes(delta, 0, 1), jnp.swapaxes(x, 0, 1), jnp.swapaxes(B_ssm, 0, 1), jnp.swapaxes(C_ssm, 0, 1))
            _, y = jax.lax.scan(step, h0, xs)
            y = jnp.swapaxes(y, 0, 1)
            y = y + x * D
            y = y * (z * jax.nn.sigmoid(z))
            return y @ W_out.T + b_out
        return _ssm_forward(u, W_in, b_in, W_x, b_x, W_dt, b_dt, A_log, D, W_out, b_out)

    def _L0_ffn_ref(x, Wg, bg, Wi, Wo, A, B):
        import jax, jax.numpy as jnp
        import numpy as np
        TOP_K = 2
        E = Wg.shape[0]
        logits = jnp.einsum('bsd,ed->bse', x, Wg) + bg
        scores = jax.nn.softmax(logits, axis=-1)
        topv, topi = jax.lax.top_k(scores, TOP_K)
        w = jnp.sum(jax.nn.one_hot(topi, E, dtype=x.dtype) * topv[..., None], axis=-2)
        base = jnp.einsum('bsd,fd->bsf', x, Wi)
        lora_low = jnp.einsum('bsd,erd->bser', x, A)
        lora = jnp.einsum('bser,efr->bsef', lora_low, B)
        h = jax.nn.relu(base[:, :, None, :] + lora)
        expert_out = jnp.einsum('bsef,df->bsed', h, Wo)
        out = jnp.einsum('bse,bsed->bsd', w, expert_out)
        return out
    x = L0_attn_u
    x = x + _L0_attn_ref(_layernorm(x, axis=-1), L0_attn_W_in, L0_attn_b_in, L0_attn_W_x, L0_attn_b_x, L0_attn_W_dt, L0_attn_b_dt, L0_attn_A_log, L0_attn_D, L0_attn_W_out, L0_attn_b_out)
    x = x + _L0_ffn_ref(_layernorm(x, axis=-1), L0_ffn_Wg, L0_ffn_bg, L0_ffn_Wi, L0_ffn_Wo, L0_ffn_A, L0_ffn_B)
    return x

_drawn_inputs = setup_inputs


def setup_inputs(seed=0):
    import zlib

    import numpy as np

    out = dict(_drawn_inputs(seed))
    spreads = {'L0_attn_D': (1.0, 0.6), 'L0_ffn_bg': (0.0, 0.8)}
    factors = {'L0_attn_b_in': 3.224,
     'L0_attn_b_x': 3.079,
     'L0_attn_W_dt': 4.777,
     'L0_attn_b_dt': 5.628,
     'L0_ffn_A': 7.725,
     'L0_ffn_B': 7.781}
    for name, (base, spread) in spreads.items():
        noise = np.random.default_rng([zlib.crc32(name.encode()), seed]).standard_normal(out[name].shape)
        drawn = base * np.exp(spread * noise) if base else spread * noise
        out[name] = jnp.asarray(drawn.astype(out[name].dtype))
    for name, factor in factors.items():
        out[name] = (out[name] * factor).astype(out[name].dtype)
    return out
```

```python
from contextlib import ExitStack

import numpy as np
import concourse.bass as bass
from concourse import mybir

F32 = mybir.dt.float32
F32R = mybir.dt.float32r
ALU = mybir.AluOpType
ACT = mybir.ActivationFunctionType
AX = mybir.AxisListType.X

P = 128
BATCH, SEQ, D = 4, 2048, 256
DI, NS, RANK = 512, 16, 16
FF, NE, LR = 1024, 4, 4
T = 512
NC = BATCH * SEQ // T
TT = T // P
KD = D // P
M = DI // P
J = P // 32
KG = NS // 4
STEPS = M * KG
UNITS = STEPS * J
NF = FF // P
NP = 2 * TT
EPS = 1e-5
BIG = 1e18

PE_SIDE = [
    ["T1 late", "J3 late", "K0 late"], ["A0 pre", "A1 pre", "T2 late", "J4 late"],
    ["B0 pre", "T3 late", "J5 late", "E0 main"], ["B1 pre", "K1 late"],
    ["B2 pre", "T4 late", "J6 late"], ["B3 pre", "T5 late", "J7 late", "K2 late"],
    ["T6 late", "C0 pre", "E1 main", "F0 post"], ["T7 late", "F1 post", "F2 post"],
    ["D0 pre", "D1 pre", "F3 post", "K3 late"], ["G0 post", "G1 post"], ["E2 main", "H0 post"], [],
    ["I0 post"], ["J0 post", "E3 main"], ["J1 post"], ["T0 post", "J2 post", "D2 pre", "D3 pre"],
]
ACT_SIDE = [
    ["S2 late", "T1 late", "J3 late"], ["R1 pre", "L1 main", "S3 late", "J4 late"],
    ["T2 late", "A0 pre", "A1 pre", "T3 late", "S4 late", "J5 late", "E0 main"], ["S5 late", "B0 pre"],
    ["B1 pre", "Z0 main", "T4 late", "J6 late"], ["S6 late", "B2 pre", "T5 late", "J7 late"],
    ["B3 pre", "S7 late", "T6 late", "E1 main"], ["C0 pre"], ["T7 late", "Z1 main", "D0 pre", "D1 pre"],
    ["R2 post"], ["L0 pre", "G0 post", "G1 post", "E2 main"], ["X0 post"], ["Z2 main"],
    ["I0 post", "J0 post", "E3 main"], ["S0 post", "J1 post"],
    ["S1 post", "T0 post", "Z3 main", "D2 pre", "D3 pre", "J2 post"],
]
DVE_SIDE = [
    ["N0 pre", "U1 main"], ["K0 late", "O0 pre", "Y3 post"], ["V1 main"], ["W0 main"], ["K1 late"], ["Y0 main"],
    ["K2 late", "F0 post"], ["F1 post", "W1 main", "C0 pre"], ["F2 post", "F3 post"],
    ["P0 post", "U0 pre", "Y1 main", "Q0 post", "K3 late"], [], ["H0 post", "V0 pre", "W2 main"], ["H1 post"],
    ["Y2 main"], ["W3 main"], [],
]
POOL_SIDE = [
    ["S3 post", "R2 late"], ["R3 late"], ["G3 post", "R4 late"], ["R5 late", "U1 main"], [],
    ["S0 main", "R6 late"], ["G0 main", "R7 late"], [], [], ["S1 main"], ["G1 main"], [],
    ["U0 pre", "B0 main"], ["S2 main"], ["G2 main", "R0 post"], ["R1 post"],
]
RINGS = {"front": ("ABCDE", 2), "up": ("FGJ", 2), "down": ("HITK", 1)}


def ring_jobs(ring):
    return [j for step in PE_SIDE for j in step if j[0] in RINGS[ring][0]]


def bank_of(ring, job):
    return ring_jobs(ring).index(job) % RINGS[ring][1]


def parts_of(c):
    got = set()
    if 0 <= c < NC:
        got.add("main")
    if c + 1 < NC:
        got.add("pre")
    if 0 <= c - 1 < NC:
        got.add("post")
    if 0 <= c - 2 < NC:
        got.add("late")
    return got


def used(ring, bank, c, job, off=0):
    def count(at):
        n = 0
        for body in range(-1, at + 1):
            for x in ring_jobs(ring):
                if x.split()[1] in parts_of(body) and bank_of(ring, x) == bank:
                    n += 1
                if body == at and x == job:
                    break
        return n

    if isinstance(c, int):
        return count(c + off)
    first, slope = count(2 + off), count(3 + off) - count(2 + off)
    assert all(count(x + off) == first + (x - 2) * slope for x in range(2, NC - 2))
    return c * slope + (first - 2 * slope)


def block_program(nc, u, w_in, b_in, w_x, b_x, w_dt, b_dt, a_log, d_skip, w_out, b_out, w_ga, b_g, w_i, w_o,
                  lora_b, ident_in, nsum_in, tri_in, out):
    with ExitStack() as ctx:
        def sb(name, shape, dt=F32):
            return ctx.enter_context(nc.sbuf_tensor(name, shape, dt))

        def sem(name):
            return ctx.enter_context(nc.semaphore(name))

        bc_dram = nc.dram_tensor("bc_scratch", (2, NS, T), F32, kind="Internal").ap()
        rep_dram = nc.dram_tensor("rep_scratch", (2, M, P, T), F32, kind="Internal").ap()

        w_in_sb = sb("w_in_sb", [P, KD, 2 * DI])
        w_x_sb = sb("w_x_sb", [P, M, P])
        w_dt_st = sb("w_dt_st", [P, DI], F32R)
        w_out_sb = sb("w_out_sb", [P, M, D])
        w_ga_sb = sb("w_ga_sb", [P, KD, NE + NE * LR])
        w_i_sb = sb("w_i_sb", [P, KD, FF])
        w_o_sb = sb("w_o_sb", [P, NF, D])
        lora_st = sb("lora_st", [P, 2, FF], F32R)
        ident = sb("ident", [P, P])
        nsum = sb("nsum", [P, 32])
        tri = sb("tri", [P, TT, NE, NE])
        b_in_sb = sb("b_in_sb", [P, 2 * M])
        nb_z = sb("nb_z", [P, M])
        b_x_sb = sb("b_x_sb", [P, 1])
        b_dt_sb = sb("b_dt_sb", [P, M])
        d_sb = sb("d_sb", [P, M])
        a_sb = sb("a_sb", [P, UNITS])
        b_out_sb = sb("b_out_sb", [P, D])
        b_g_sb = sb("b_g_sb", [P, TT, NE])
        xin = sb("xin", [P, TT, D])
        xn_t = [sb(f"xn_t{i}", [P, KD, T]) for i in range(2)]
        x_t = [sb(f"x_t{i}", [P, M, T]) for i in range(2)]
        dbc = sb("dbc", [P, T])
        dt_st = sb("dt_st", [P, T], F32R)
        z_dt = sb("z_dt", [P, 2, T])
        e_dt = sb("e_dt", [P, 2, T])
        z_gate = [sb(f"z_gate{i}", [P, T]) for i in range(2)]
        e_gate = sb("e_gate", [P, T])
        gated = [sb(f"gated{i}", [P, M, T]) for i in range(2)]
        b_rep = sb("b_rep", [P, KG, T])
        c_rep = sb("c_rep", [P, KG, T])
        dt_rep = [sb(f"dt_rep{i}", [P, J, T]) for i in range(2)]
        dx_rep = [sb(f"dx_rep{i}", [P, J, T]) for i in range(2)]
        hs = [sb(f"hs{i}", [P, J, T]) for i in range(4)]
        state = [sb(f"state{i}", [P, UNITS]) for i in range(2)]
        state_next = [sb(f"state_next{i}", [P, UNITS]) for i in range(2)]
        xr = sb("xr", [P, TT, D])
        x1 = [sb(f"x1_{i}", [P, TT, D]) for i in range(2)]
        x2_t = sb("x2_t", [P, KD, T])
        low_t = sb("low_t", [P, T], F32R)
        r1 = [sb(f"r1_{i}", [P, T]) for i in range(2)]
        r2 = [sb(f"r2_{i}", [P, T]) for i in range(2)]
        r_t = sb("r_t", [P, NF, P])
        st1 = sb("st1", [P, TT, 6])
        mv1 = sb("mv1", [P, TT, 2])
        ve1 = sb("ve1", [P, TT])
        rs1 = sb("rs1", [P, TT])
        nt1 = sb("nt1", [P, TT])
        st2 = sb("st2", [P, TT, 6])
        mv2 = sb("mv2", [P, TT, 2])
        ve2 = sb("ve2", [P, TT])
        rs2 = sb("rs2", [P, TT])
        nt2 = sb("nt2", [P, TT])
        lg = sb("lg", [P, TT, NE])
        low = sb("low", [P, TT, NE * LR])
        mx = sb("mx", [P, TT])
        lm = sb("lm", [P, TT, NE])
        pexp = sb("pexp", [P, TT, NE])
        sm = sb("sm", [P, TT])
        rsm = sb("rsm", [P, TT])
        sc = sb("sc", [P, TT, NE])
        gt = sb("gt", [P, TT, NE, NE])
        eq = sb("eq", [P, TT, NE, NE])
        rank = sb("rank", [P, TT, NE])
        sel = sb("sel", [P, 2, TT, NE])
        wk = sb("wk", [P, 2, TT, NE])
        wgt = sb("wgt", [P, 2, TT])
        msk = sb("msk", [P, 2, TT, NE, LR])
        msk_hi = sb("msk_hi", [P, 2, TT, NE * LR], F32R)
        pk = sb("pk", [P, TT, 2, 2, 2, NE * LR])

        decay = [ctx.enter_context(nc.psum_tensor(f"decay{i}", [P, T], F32)) for i in range(2)]
        y_ps = ctx.enter_context(nc.psum_tensor("y_ps", [P, T], F32))
        banks = {r: [ctx.enter_context(nc.psum_tensor(f"{r}{i}", [P, 512], F32)) for i in range(RINGS[r][1])]
                 for r in RINGS}
        filled = {r: [sem(f"{r}_filled{i}") for i in range(RINGS[r][1])] for r in RINGS}
        freed = {r: [sem(f"{r}_freed{i}") for i in range(RINGS[r][1])] for r in RINGS}

        (w_loaded, zeroed, a_ready, raw_rounded, weights_split, xin_loaded, ln1_part, ln1_root, ln1_newton, xn_ready,
         dt_hi, dt_lo, clamp_dt, log_dt, delta_ready, dx_ready, bc_stored, rep_stored) = (sem(n) for n in (
            "w_loaded", "zeroed", "a_ready", "raw_rounded", "weights_split", "xin_loaded", "ln1_part", "ln1_root",
            "ln1_newton", "xn_ready", "dt_hi", "dt_lo", "clamp_dt", "log_dt", "delta_ready", "dx_ready",
            "bc_stored", "rep_stored"))
        rep_loaded = [sem(f"rep_loaded{i}") for i in range(2)]
        b_loaded = [sem(f"b_loaded{k}") for k in range(KG)]
        c_loaded = [sem(f"c_loaded{k}") for k in range(KG)]
        (decay_ready, input_ready, scan_done, state_moved, state_kept, prod_ready, nsum_done, y_read, gated_ready,
         clamp_z, log_z, sig_ready, silu_ready) = (sem(n) for n in (
            "decay_ready", "input_ready", "scan_done", "state_moved", "state_kept", "prod_ready", "nsum_done", "y_read",
            "gated_ready", "clamp_z", "log_z", "sig_ready", "silu_ready"))
        (xr_loaded, xr_ready, ln2_part, ln2_root, ln2_newton, x2_ready, router, router_exp, masks_ready, r1_ready,
         z2_ready, r_ready) = (sem(n) for n in (
            "xr_loaded", "xr_ready", "ln2_part", "ln2_root", "ln2_newton", "x2_ready", "router", "router_exp",
            "masks_ready", "r1_ready", "z2_ready", "r_ready"))
        sp_turn = sem("sp_turn")
        router_step, mask_split = sem("router_step"), sem("mask_split")
        R_STEPS = 13
        out_stored = [sem(f"out_stored{t}") for t in range(TT)]

        block = ctx.enter_context(nc.Block())

        def at_least(eng, s, value):
            if not (isinstance(value, int) and value <= 0):
                eng.wait_ge(s, value)

        def chunk_of(c, when):
            return c + {"pre": 1, "main": 0, "post": -1, "late": -2}[when]

        def odd_of(par, when):
            return (par + {"pre": 1, "main": 0, "post": 1, "late": 0}[when]) % 2

        def ring_of(job):
            ring = next(r for r in RINGS if job[0] in RINGS[r][0])
            return ring, bank_of(ring, job)

        def tile_job(i):
            return next(j for j in ring_jobs("up") if j.startswith(f"J{i}"))

        def wait_filled(eng, job, c):
            ring, b = ring_of(job)
            eng.wait_ge(filled[ring][b], used(ring, b, c, job))
            return banks[ring][b], freed[ring][b]

        def wait_read(eng, job, c, off=0):
            ring, b = ring_of(job)
            eng.wait_ge(freed[ring][b], used(ring, b, c, job, off))

        def sweep(eng, body):
            for c in (-1, 0, 1):
                body(c, c % 2, parts_of(c))
            with eng.Fori(1, (NC - 2) // 2) as pair:
                for odd in range(2):
                    body(pair * 2 + odd, odd, parts_of(2))
            for c in (NC - 2, NC - 1, NC, NC + 1):
                body(c, c % 2, parts_of(c))

        def side(table, s, parts):
            for job in table[s]:
                if job.split()[1] in parts:
                    yield job[0], int(job[1]), job.split()[1], job

        loads = ((xin[:], u[0].rearrange("(t p) d -> p t d", p=P)),
                 (w_in_sb[:], w_in), (b_in_sb[:], b_in), (nb_z[:], b_in[:, M:2 * M]), (ident[:], ident_in),
                 (w_x_sb[:], w_x), (b_x_sb[:], b_x), (hs[1][:, 0, :], w_dt), (b_dt_sb[:], b_dt),
                 (hs[2][:].rearrange("p a t -> p (a t)").rearrange("p (a t) -> p a t", a=2), lora_b),
                 (a_sb[:], a_log), (d_sb[:], d_skip), (nsum[:], nsum_in), (w_out_sb[:], w_out),
                 (w_ga_sb[:], w_ga), (tri[:], tri_in), (b_g_sb[:], b_g), (b_out_sb[:], b_out),
                 (w_i_sb[:], w_i), (w_o_sb[:], w_o))

        @block.sync
        def _(sp):
            for n, (dst, src) in enumerate(loads):
                sp.dma_start(dst, src).then_inc(xin_loaded if n == 0 else w_loaded, 16)

            def load_rep(c, m):
                for kind, dst in enumerate((dt_rep, dx_rep)):
                    for n in range(4):
                        sp.dma_start(dst[m % 2][32 * n:32 * n + 32, :, :],
                                     rep_dram[kind, m].rearrange("(j d) t -> d j t", j=J)).then_inc(rep_loaded[m % 2], 16)

            def load_bc(which, k):
                dst, s = ((b_rep, b_loaded), (c_rep, c_loaded))[which]
                for n in range(4):
                    sp.dma_start(dst[32 * n:32 * n + 32, k, :],
                                 bc_dram[which, 4 * k + n:4 * k + n + 1, :].to_broadcast([32, T])).then_inc(s[k], 16)

            def waits(*needs):
                for s_, at in needs:
                    at_least(sp, s_, at)
                    if not isinstance(at, int):
                        sp.sem_inc(sp_turn, 1)

            def filled_by(job, c):
                ring, b = ring_of(job)
                return filled[ring][b], used(ring, b, c, job)

            def read_by(job, c):
                ring, b = ring_of(job)
                return freed[ring][b], used(ring, b, c, job)

            def store_rep(c, pair):
                back = [(rep_loaded[i], 256 * c - (128 if pair == 0 else 0)) for i in range(2)]
                waits(*back, (delta_ready, 2 * c + pair + 1), (dx_ready, 2 * c + pair + 1))
                for kind, src in enumerate((e_dt, z_dt)):
                    sp.dma_start(rep_dram[kind, 2 * pair:2 * pair + 2].rearrange("m p t -> p m t"),
                                 src[:]).then_inc(rep_stored, 16)

            def chunk_rows(dram, c):
                return dram[bass.ds(c, 1)]

            def store_out(c, par, t):
                dst = chunk_rows(out, c - 2)
                waits(read_by(f"K{t} late", c))
                sp.dma_start(dst[:, t * P:(t + 1) * P, :].rearrange("o p d -> p (o d)"),
                             x1[par][:, t, :]).then_inc(out_stored[t], 16)

            def body(c, par, parts):
                def past(m):
                    return (decay_ready, UNITS * c + KG * J * m), (input_ready, 2 * (STEPS * c + KG * m))

                for s in range(STEPS):
                    m, k = divmod(s, KG)
                    if "main" in parts and s == 0:
                        waits((prod_ready, STEPS * c))
                        load_bc(1, KG - 1)
                    if "main" in parts and k == 1 and m + 1 < M:
                        waits(*past(m), (rep_stored, 64 * c + 32 * (2 if m >= 1 else 1)))
                        load_rep(c, m + 1)
                    if "pre" in parts and s == 2 and (not isinstance(c, int) or c + 2 < NC):
                        src = chunk_rows(u, c + 2)
                        waits(filled_by("A1 pre", c))
                        sp.dma_start(xin[:], src.rearrange("o (t p) d -> p (o t) d", p=P)).then_inc(xin_loaded, 16)
                    if "main" in parts and s == 4:
                        store_rep(c, 1)
                    if "late" in parts and s in (3, 5, 7, 11):
                        store_out(c, par, (3, 5, 7, 11).index(s))
                    if "pre" in parts and s == 8:
                        back = [(x[kk], 64 * (c + 1)) for kk in range(KG) for x in (b_loaded, c_loaded)]
                        waits(read_by("C0 pre", c), *back)
                        sp.dma_start(bc_dram[0], dbc[16:32, :]).then_inc(bc_stored, 16)
                        sp.dma_start(bc_dram[1], dbc[48:64, :]).then_inc(bc_stored, 16)
                    if "main" in parts and s == 11:
                        src = chunk_rows(u, c)
                        if "post" in parts:
                            waits(filled_by("G1 post", c))
                        sp.dma_start(xr[:], src.rearrange("o (t p) d -> p (o t) d", p=P)).then_inc(xr_loaded, 16)
                    if "pre" in parts and s == 13:
                        store_rep(c + 1, 0)
                        waits((rep_stored, 64 * (c + 1) + 32), *past(M - 1))
                        load_rep(c + 1, 0)
                    if "pre" in parts and s >= 12:
                        if s == 12:
                            waits((bc_stored, 32 * (c + 2)))
                        waits((input_ready, 2 * (STEPS * c + s + 1)))
                        load_bc(0, s - 12)
                        if s > 12:
                            waits((prod_ready, STEPS * c + s))
                            load_bc(1, s - 13)

            sweep(sp, body)
            for t in range(TT):
                sp.wait_ge(out_stored[t], 16 * NC)

        @block.tensor
        def _(pe):
            pe.wait_ge(w_loaded, 16 * (len(loads) - 1))
            pe.wait_ge(weights_split, 2)

            def job_pe(letter, i, when, job, c, par):
                q, odd = chunk_of(c, when), odd_of(par, when)
                ring, b = ring_of(job)
                ps = banks[ring][b]
                at_least(pe, freed[ring][b], used(ring, b, c, job) - 1)

                def needs(other):
                    if ring_of(other) != (ring, b):
                        wait_read(pe, other, c)

                if letter in "AG":
                    pe.wait_ge(xn_ready if letter == "A" else x2_ready, q + 1)
                    src = xin if letter == "A" else xr
                    for t in range(TT):
                        mm = pe.transpose(ps[:, t * P:(t + 1) * P], src[:, t, i * P:(i + 1) * P], ident[:])
                elif letter in "BE":
                    if letter == "B":
                        for k in range(KD):
                            needs(f"A{k} pre")
                    col = i * P + (DI if letter == "E" else 0)
                    for k in range(KD):
                        mm = pe.matmul(ps[:], w_in_sb[:, k, col:col + P], xn_t[odd][:, k, :], start=k == 0, stop=k == KD - 1)
                elif letter == "C":
                    for k in range(M):
                        needs(f"B{k} pre")
                        mm = pe.matmul(ps[:], w_x_sb[:, k, :], x_t[odd][:, k, :], start=k == 0, stop=k == M - 1)
                elif letter == "D":
                    pe.wait_ge(dt_lo, q + 1)
                    mm = pe.matmul(ps[:], w_dt_st[:, i * P:(i + 1) * P], dt_st[:], start=True, stop=True)
                elif letter == "F":
                    pe.wait_ge(gated_ready, M * (q + 1))
                    for k in range(M):
                        mm = pe.matmul(ps[:, 0:D], gated[odd][:, k, i * P:(i + 1) * P], w_out_sb[:, k, :], start=k == 0, stop=k == M - 1)
                elif letter == "H":
                    w = NE + NE * LR
                    for k in range(KD):
                        needs(f"G{k} post")
                    for t in range(TT):
                        for k in range(KD):
                            mm = pe.matmul(ps[:, t * w:(t + 1) * w], x2_t[:, k, t * P:(t + 1) * P], w_ga_sb[:, k, :],
                                           start=k == 0, stop=k == KD - 1)
                elif letter == "I":
                    pe.wait_ge(masks_ready, q + 1)
                    for t in range(TT):
                        mm = pe.transpose(ps[:, t * P:(t + 1) * P], pk[:, t].rearrange("p a b c d -> p (a b c d)"), ident[:])
                elif letter == "J":
                    t, half = divmod(i, 2)
                    cols = slice(half * 512, (half + 1) * 512)
                    for k in range(KD):
                        pe.matmul(ps[:], x2_t[:, k, t * P:(t + 1) * P], w_i_sb[:, k, cols], start=k == 0, stop=False)
                    if job == "J0 post":
                        needs("I0 post")
                    mm = pe.matmul(ps[:], low_t[:, t * P:(t + 1) * P], lora_st[:, 0, cols], start=False, stop=True)
                elif letter == "T":
                    pe.wait_ge(r_ready, NP * q + i + 1)
                    for f in range(4):
                        mm = pe.transpose(ps[:, f * P:(f + 1) * P], r1[i % 2][:, f * P:(f + 1) * P], ident[:])
                elif letter == "K":
                    for f in range(NF):
                        mm = pe.matmul(ps[:, 0:D], r_t[:, f, :], w_o_sb[:, f, :], start=f == 0, stop=f == NF - 1)
                mm.then_inc(filled[ring][b], 1)

            def second_choice(i, job, q):
                t, half = divmod(i, 2)
                ring, b = ring_of(job)
                pe.wait_ge(r1_ready, NP * q + i + 1)
                pe.matmul(banks[ring][b][:], low_t[:, t * P:(t + 1) * P], lora_st[:, 1, half * 512:(half + 1) * 512],
                          start=False, stop=True, skip_group_check=True).then_inc(z2_ready, 1)

            def sum_states(c, s):
                m, k = divmod(s, KG)
                pe.wait_ge(prod_ready, STEPS * c + s + 1)
                if k == 0:
                    at_least(pe, y_read, M * c + m)
                for j in range(J):
                    mm = pe.matmul(y_ps[32 * j:32 * j + 32, :], nsum[:], hs[s % 4][:, j, :], start=k == 0,
                                   stop=k == KG - 1)
                mm.then_inc(nsum_done, 1)

            def body(c, par, parts):
                for s in range(STEPS):
                    if s >= 2 and "main" in parts:
                        sum_states(c, s - 2)
                    if s < 2 and "post" in parts:
                        sum_states(c - 1, STEPS - 2 + s)
                    second = []
                    for letter, i, when, job in side(PE_SIDE, s, parts):
                        job_pe(letter, i, when, job, c, par)
                        if letter == "J":
                            second.append((i, job, chunk_of(c, when)))
                    for i, job, q in second:
                        second_choice(i, job, q)

            sweep(pe, body)

        @block.scalar
        def _(act):
            nc.scalar.preload_act_table_set("natural_log_exp_and_others")
            act.wait_ge(w_loaded, 16 * (len(loads) - 1))
            nc.scalar.activation(a_sb[:], a_sb[:], ACT.Exp).then_inc(a_ready, 1)
            act.wait_ge(a_ready, 1)
            nc.scalar.mul(a_sb[:], a_sb[:], -1.0).then_inc(a_ready, 1)
            nc.scalar.mul(nb_z[:], nb_z[:], -1.0).then_inc(a_ready, 1)
            act.wait_ge(a_ready, 3)

            def job_act(letter, i, when, job, c, par):
                q, odd = chunk_of(c, when), odd_of(par, when)
                big = not isinstance(q, int)
                if letter == "A":
                    ps, free = wait_filled(act, job, c)
                    nc.scalar.copy(xn_t[odd][:, i, :], ps[:]).then_inc(free, 1)
                elif letter == "B":
                    at_least(act, y_read, M * (q - 2) + i + 1 if big or q >= 2 else 0)
                    at_least(act, dx_ready, 2 * (q - 1) if big or q >= 2 else 0)
                    ps, free = wait_filled(act, job, c)
                    nc.scalar.activation(x_t[odd][:, i, :], ps[:], ACT.Identity, bias=b_in_sb[:, i:i + 1]).then_inc(free, 1)
                elif letter == "C":
                    at_least(act, bc_stored, 32 * q)
                    at_least(act, dt_lo, q)
                    ps, free = wait_filled(act, job, c)
                    nc.scalar.activation(dbc[:], ps[:], ACT.Identity, bias=b_x_sb[:, 0:1]).then_inc(free, 1)
                    wait_read(act, job, c)
                    nc.scalar.activation(dt_st[:], dbc[:], ACT.Identity).then_inc(dt_hi, 1)
                elif letter == "D":
                    if i % 2 == 0:
                        at_least(act, rep_stored, 64 * q + 32 * (i // 2))
                    ps, free = wait_filled(act, job, c)
                    nc.scalar.activation(z_dt[:, i % 2, :], ps[:], ACT.Identity, bias=b_dt_sb[:, i:i + 1])
                    nc.scalar.activation(e_dt[:, i % 2, :], ps[:], ACT.Exp, bias=b_dt_sb[:, i:i + 1]).then_inc(free, 1)
                elif letter == "L":
                    act.wait_ge(clamp_dt, 2 * q + i + 1)
                    nc.scalar.activation(e_dt[:], e_dt[:], ACT.Ln).then_inc(log_dt, 1)
                elif letter == "E":
                    at_least(act, gated_ready, M * q + i - 1)
                    ps, free = wait_filled(act, job, c)
                    nc.scalar.activation(z_gate[i % 2][:], ps[:], ACT.Identity, bias=b_in_sb[:, M + i:M + i + 1])
                    at_least(act, silu_ready, M * q + i)
                    nc.scalar.activation(e_gate[:], ps[:], ACT.Exp, scale=-1.0, bias=nb_z[:, i:i + 1]).then_inc(free, 1)
                elif letter == "Z":
                    act.wait_ge(clamp_z, M * q + i + 1)
                    nc.scalar.activation(e_gate[:], e_gate[:], ACT.Ln).then_inc(log_z, 1)
                    act.wait_ge(log_z, M * q + i + 1)
                    nc.scalar.activation(e_gate[:], e_gate[:], ACT.Exp, scale=-1.0).then_inc(sig_ready, 1)
                elif letter == "R":
                    ve, rs, part, root = (ve1, rs1, ln1_part, ln1_root) if i == 1 else (ve2, rs2, ln2_part, ln2_root)
                    act.wait_ge(part, 3 * (q + 1))
                    nc.scalar.activation(rs[:], ve[:], ACT.Ln).then_inc(root, 1)
                    act.wait_ge(root, 2 * q + 1)
                    nc.scalar.activation(rs[:], rs[:], ACT.Exp, scale=-0.5).then_inc(root, 1)
                elif letter == "G":
                    ps, free = wait_filled(act, job, c)
                    nc.scalar.copy(x2_t[:, i, :], ps[:]).then_inc(free, 1)
                elif letter == "X":
                    act.wait_ge(router, q + 1)
                    nc.scalar.activation(pexp[:], lm[:], ACT.Exp).then_inc(router_exp, 1)
                elif letter == "I":
                    ps, free = wait_filled(act, job, c)
                    nc.scalar.activation(low_t[:], ps[:], ACT.Identity).then_inc(free, 1)
                elif letter == "J":
                    ps, _ = wait_filled(act, job, c)
                    nc.scalar.activation(r1[i % 2][:], ps[:], ACT.Relu, scale=wgt[:, 0, i // 2:i // 2 + 1]).then_inc(r1_ready, 1)
                elif letter == "S":
                    at_least(act, r_ready, NP * q + i - 1)
                    act.wait_ge(z2_ready, NP * q + i + 1)
                    ring, b = ring_of(tile_job(i))
                    nc.scalar.activation(r2[i % 2][:], banks[ring][b][:], ACT.Relu,
                                         scale=wgt[:, 1, i // 2:i // 2 + 1]).then_inc(freed[ring][b], 1)
                elif letter == "T":
                    ps, free = wait_filled(act, job, c)
                    nc.scalar.copy(r_t[:, 4 * (i % 2):4 * (i % 2) + 4, :].rearrange("p f t -> p (f t)"), ps[:]).then_inc(free, 1)

            def body(c, par, parts):
                for s in range(STEPS):
                    m, k = divmod(s, KG)
                    jobs = list(side(ACT_SIDE, s, parts))
                    for j in range(J):
                        if "main" in parts:
                            n = UNITS * c + J * s + j
                            if j == 0 and k == 0:
                                act.wait_ge(rep_loaded[m % 2], 256 * c + 128 * (m // 2 + 1))
                            at_least(act, scan_done, n - 1)
                            nc.scalar.activation(decay[j % 2][:], dt_rep[m % 2][:, j, :], ACT.Exp,
                                                 scale=a_sb[:, J * s + j:J * s + j + 1]).then_inc(decay_ready, 1)
                        if j in (1, 2) and s >= 1 and "main" in parts:
                            (move_state, keep_state)[j - 1](c, par, s - 1)
                        if j in (1, 2) and s == 0 and "post" in parts:
                            (move_state, keep_state)[j - 1](c - 1, 1 - par, STEPS - 1)
                        for job in jobs[len(jobs) * j // J:len(jobs) * (j + 1) // J]:
                            job_act(*job, c, par)

            def move_state(c, par, s):
                cols = slice(J * s, J * s + J)
                act.wait_ge(scan_done, UNITS * c + J * (s + 1))
                nc.scalar.copy(state[par][:, cols], state_next[par][:, cols]).then_inc(state_moved, 1)

            def keep_state(c, par, s):
                act.wait_ge(state_moved, STEPS * c + s + 1)
                nc.scalar.copy(state_next[par][:, J * s:J * s + J], hs[s % 4][:, :, T - 1]).then_inc(state_kept, 1)

            sweep(act, body)

        @block.vector
        def _(dve):
            v = nc.vector
            for par in range(2):
                v.memset(state[par][:], 0.0)
                v.memset(state_next[par][:], 0.0).then_inc(zeroed, 1)
            dve.wait_ge(w_loaded, 16 * (len(loads) - 1))
            raw_lora = hs[2][:].rearrange("p a t -> p (a t)").rearrange("p (a t) -> p a t", a=2)
            v.tensor_copy(w_dt_st[:], hs[1][:, 0, :])
            v.tensor_copy(lora_st[:], raw_lora).then_inc(raw_rounded, 1)
            dve.wait_ge(raw_rounded, 1)
            for st, raw in ((w_dt_st, hs[1][:, 0, :]), (lora_st, raw_lora)):
                for lo in (32, 96):
                    last = v.tensor_tensor(st[lo:lo + 32], raw[lo:lo + 32], st[lo:lo + 32].bitcast(F32), ALU.subtract)
                last.then_inc(weights_split, 1)
            dve.wait_ge(weights_split, 2)

            def stats(q, src, st, mv, ve, part):
                for t in range(TT):
                    last = v.bn_stats(st[:, t, :], src[:, t, :])
                last.then_inc(part, 1)
                dve.wait_ge(part, 3 * q + 1)
                v.memset(ve[:], EPS)
                for t in range(TT):
                    last = v.bn_aggr(mv[:, t, :], st[:, t, :])
                last.then_inc(part, 1)
                dve.wait_ge(part, 3 * q + 2)
                v.tensor_tensor(ve[:], mv[:, :, 1], ve[:], ALU.add).then_inc(part, 1)

            def normalise(q, dst, src, mv, ve, rs, nt, part, root, newton, done):
                dve.wait_ge(root, 2 * (q + 1))
                v.tensor_tensor(nt[:], rs[:], rs[:], ALU.mult).then_inc(newton, 1)
                dve.wait_ge(newton, 4 * q + 1)
                v.tensor_tensor(nt[:], nt[:], ve[:], ALU.mult).then_inc(newton, 1)
                dve.wait_ge(newton, 4 * q + 2)
                v.tensor_scalar(nt[:], nt[:], -0.5, 1.5, ALU.mult, ALU.add).then_inc(newton, 1)
                dve.wait_ge(newton, 4 * q + 3)
                v.tensor_tensor(rs[:], rs[:], nt[:], ALU.mult).then_inc(newton, 1)
                dve.wait_ge(newton, 4 * q + 4)
                for t in range(TT):
                    last = v.tensor_scalar(dst[:, t, :], src[:, t, :], mv[:, t, 0:1], rs[:, t:t + 1], ALU.subtract, ALU.mult)
                last.then_inc(done, 1)

            def job_dve(letter, i, when, job, c, par):
                q, odd = chunk_of(c, when), odd_of(par, when)
                if letter == "N":
                    dve.wait_ge(xin_loaded, 16 * (q + 1))
                    stats(q, xin, st1, mv1, ve1, ln1_part)
                elif letter == "O":
                    normalise(q, xin, xin, mv1, ve1, rs1, nt1, ln1_part, ln1_root, ln1_newton, xn_ready)
                elif letter == "P":
                    for t in range(TT - 2, TT):
                        wait_read(dve, f"F{t} post", c)
                    stats(q, x1[odd], st2, mv2, ve2, ln2_part)
                elif letter == "Q":
                    normalise(q, xr, x1[odd], mv2, ve2, rs2, nt2, ln2_part, ln2_root, ln2_newton, x2_ready)
                elif letter == "C":
                    dve.wait_ge(dt_hi, q + 1)
                    v.tensor_tensor(dt_st[64:128], dbc[64:128], dt_st[64:128].bitcast(F32), ALU.subtract).then_inc(dt_lo, 1)
                elif letter == "U":
                    for n in (2 * i, 2 * i + 1):
                        if when == "pre":
                            wait_read(dve, f"D{n} pre", c)
                        else:
                            wait_read(dve, f"D{n} pre", c, -1)
                    v.tensor_scalar(e_dt[:], e_dt[:], BIG, 1.0, ALU.min, ALU.add).then_inc(clamp_dt, 1)
                elif letter == "V":
                    dve.wait_ge(log_dt, 2 * q + i + 1)
                    v.tensor_tensor(e_dt[:], e_dt[:], z_dt[:], ALU.max).then_inc(delta_ready, 1)
                elif letter == "W":
                    wait_read(dve, f"E{i} main", c)
                    v.tensor_scalar(e_gate[:], e_gate[:], BIG, 1.0, ALU.min, ALU.add).then_inc(clamp_z, 1)
                elif letter == "Y":
                    dve.wait_ge(nsum_done, STEPS * q + KG * (i + 1))
                    v.scalar_tensor_tensor(out=gated[odd][:, i, :], in0=x_t[odd][:, i, :], scalar=d_sb[:, i:i + 1],
                                           in1=y_ps[:], op0=ALU.mult, op1=ALU.add).then_inc(y_read, 1)
                elif letter == "F":
                    if i == 0:
                        dve.wait_ge(xr_ready, q + 1)
                    at_least(dve, out_stored[i], 16 * (q - 1))
                    ps, free = wait_filled(dve, job, c)
                    v.tensor_tensor(x1[odd][:, i, :], ps[:, 0:D], xr[:, i, :], ALU.add).then_inc(free, 1)
                elif letter == "K":
                    ps, free = wait_filled(dve, job, c)
                    v.tensor_tensor(x1[odd][:, i, :], ps[:, 0:D], x1[odd][:, i, :], ALU.add).then_inc(free, 1)
                elif letter == "H" and i == 0:
                    ps, free = wait_filled(dve, job, c)
                    z = ps[:, 0:TT * (NE + NE * LR)].rearrange("p (t w) -> p t w", t=TT)
                    v.tensor_tensor(lg[:], z[:, :, 0:NE], b_g_sb[:], ALU.add).then_inc(router_step, 1)
                    v.tensor_copy(low[:], z[:, :, NE:]).then_inc(free, 1)
                    dve.wait_ge(router_step, R_STEPS * q + 1)
                    v.tensor_reduce(mx[:], lg[:], AX, ALU.max).then_inc(router_step, 1)
                    dve.wait_ge(router_step, R_STEPS * q + 2)
                    v.tensor_tensor(lm[:], lg[:], mx[:].unsqueeze(2).to_broadcast([P, TT, NE]), ALU.subtract).then_inc(router, 1)
                elif letter == "H":
                    choose(q)

            def choose(q):
                base = R_STEPS * q

                def then(n, ins):
                    ins.then_inc(router_step, 1)
                    dve.wait_ge(router_step, base + n)

                dve.wait_ge(router_exp, q + 1)
                then(3, v.tensor_reduce(sm[:], pexp[:], AX, ALU.add))
                then(4, v.reciprocal(rsm[:], sm[:]))
                then(5, v.tensor_tensor(sc[:], pexp[:], rsm[:].unsqueeze(2).to_broadcast([P, TT, NE]), ALU.mult))
                other = sc[:].unsqueeze(2).to_broadcast([P, TT, NE, NE])
                own = sc[:].unsqueeze(3).to_broadcast([P, TT, NE, NE])
                v.tensor_tensor(gt[:], other, own, ALU.is_gt)
                then(6, v.tensor_tensor(eq[:], other, own, ALU.is_equal))
                then(7, v.tensor_tensor(eq[:], eq[:], tri[:], ALU.mult))
                then(8, v.tensor_tensor(gt[:], gt[:], eq[:], ALU.add))
                then(9, v.tensor_reduce(rank[:], gt[:], AX, ALU.add))
                v.tensor_scalar(sel[:, 0], rank[:], 0.0, None, ALU.is_equal)
                then(10, v.tensor_scalar(sel[:, 1], rank[:], 1.0, None, ALU.is_equal))
                for a in range(2):
                    last = v.tensor_tensor(wk[:, a], sel[:, a], sc[:], ALU.mult)
                then(11, last)
                v.tensor_reduce(wgt[:], wk[:], AX, ALU.add)
                v.tensor_tensor(sel[:, 1], sel[:, 1], sel[:, 0], ALU.subtract).then_inc(router_step, 1)
                dve.wait_ge(router_step, base + 12)
                lw = low[:].rearrange("p t (e r) -> p t e r", e=NE)
                for a in range(2):
                    last = v.tensor_tensor(msk[:, a], lw, sel[:, a].unsqueeze(3).to_broadcast([P, TT, NE, LR]), ALU.mult)
                then(13, last)
                flat = msk[:].rearrange("p a t e r -> p a t (e r)")
                v.tensor_copy(msk_hi[:], flat).then_inc(mask_split, 1)
                dve.wait_ge(mask_split, q + 1)
                hi = msk_hi[:].bitcast(F32)
                for a in range(2):
                    for copy in range(2):
                        v.tensor_copy(pk[:, :, a, copy, 0], hi[:, a])
                        last = v.tensor_tensor(pk[:, :, a, copy, 1], flat[:, a], hi[:, a], ALU.subtract)
                last.then_inc(masks_ready, 1)

            def scan_input(c, par, s, half):
                m, k = divmod(s, KG)
                if half == 0:
                    if k == 0:
                        dve.wait_ge(rep_loaded[m % 2], 256 * c + 128 * (m // 2 + 1))
                    if m == 0:
                        dve.wait_ge(b_loaded[k], 64 * (c + 1))
                    at_least(dve, nsum_done, STEPS * c + s - 3)
                js = slice(2 * half, 2 * half + 2)
                v.tensor_tensor(hs[s % 4][:, js, :], dx_rep[m % 2][:, js, :],
                                b_rep[:, k, :].unsqueeze(1).to_broadcast([P, 2, T]), ALU.mult).then_inc(input_ready, 1)

            def body(c, par, parts):
                for s in range(STEPS):
                    jobs = list(side(DVE_SIDE, s, parts))
                    for j in range(J):
                        if "main" in parts and j % 2 == 0:
                            if s + 1 < STEPS:
                                scan_input(c, par, s + 1, j // 2)
                            elif "pre" in parts:
                                scan_input(c + 1, 1 - par, 0, j // 2)
                            dve.wait_ge(input_ready, 2 * (STEPS * c + s) + j // 2 + 1)
                        if "main" in parts:
                            dve.wait_ge(decay_ready, UNITS * c + J * s + j + 1)
                            h = hs[s % 4][:, j, :]
                            v.tensor_tensor_scan(h, decay[j % 2][:], h, state[par][:, J * s + j:J * s + j + 1],
                                                 ALU.mult, ALU.add).then_inc(scan_done, 1)
                        for job in [x for i, x in enumerate(jobs) if i * J // len(jobs) == j]:
                            job_dve(*job, c, par)
                if "main" not in parts and "pre" in parts:
                    for half in range(2):
                        scan_input(0, 0, 0, half)

            sweep(dve, body)

        @block.gpsimd
        def _(pool):
            pool.wait_ge(w_loaded, 16 * (len(loads) - 1))

            def job_pool(letter, i, when, job, c, par):
                q, odd = chunk_of(c, when), odd_of(par, when)
                g = nc.gpsimd
                if letter == "U":
                    pool.wait_ge(delta_ready, 2 * q + i + 1)
                    g.tensor_tensor(z_dt[:], e_dt[:], x_t[odd][:, 2 * i:2 * i + 2, :], ALU.mult).then_inc(dx_ready, 1)
                elif letter == "S":
                    pool.wait_ge(sig_ready, M * q + i + 1)
                    g.tensor_tensor(z_gate[i % 2][:], z_gate[i % 2][:], e_gate[:], ALU.mult).then_inc(silu_ready, 1)
                elif letter == "G":
                    pool.wait_ge(y_read, M * q + i + 1)
                    pool.wait_ge(silu_ready, M * q + i + 1)
                    g.tensor_tensor(gated[odd][:, i, :], gated[odd][:, i, :], z_gate[i % 2][:], ALU.mult).then_inc(gated_ready, 1)
                elif letter == "B":
                    pool.wait_ge(xr_loaded, 16 * (q + 1))
                    g.tensor_tensor(xr[:], xr[:], b_out_sb[:].unsqueeze(1).to_broadcast([P, TT, D]), ALU.add).then_inc(xr_ready, 1)
                elif letter == "R":
                    name = tile_job(i)
                    wait_read(pool, name, c, -1 if name.split()[1] == "post" and when == "late" else 0)
                    g.tensor_tensor(r1[i % 2][:], r1[i % 2][:], r2[i % 2][:], ALU.add).then_inc(r_ready, 1)

            def times_c(c, s):
                k = s % KG
                pool.wait_ge(scan_done, UNITS * c + J * (s + 1))
                pool.wait_ge(state_kept, STEPS * c + s + 1)
                if s < KG:
                    pool.wait_ge(c_loaded[k], 64 * (c + 1))
                nc.gpsimd.tensor_tensor(hs[s % 4][:], hs[s % 4][:], c_rep[:, k, :].unsqueeze(1).to_broadcast([P, J, T]),
                                        ALU.mult).then_inc(prod_ready, 1)

            def body(c, par, parts):
                for s in range(STEPS):
                    if s >= 1 and "main" in parts:
                        times_c(c, s - 1)
                    if s == 0 and "post" in parts:
                        times_c(c - 1, STEPS - 1)
                    for job in side(POOL_SIDE, s, parts):
                        job_pool(*job, c, par)

            sweep(pool, body)


def kernel(**inputs):
    import numpy as _np
    import concourse.bacc as _bacc
    from concourse import mybir as _mybir
    from concourse.bass_utils import run_bass_kernel_spmd as _run

    x = {k: _np.asarray(a) for k, a in inputs.items()}
    f32 = _np.float32

    def blocks(a):
        return a.reshape(-1, P, a.shape[-1]).transpose(1, 0, 2)

    u = x["L0_attn_u"].reshape(BATCH, SEQ // T, T, D).transpose(1, 0, 2, 3).reshape(NC, T, D)
    wx, bx = x["L0_attn_W_x"], x["L0_attn_b_x"]
    w_x, b_x = _np.zeros((P, DI), f32), _np.zeros((P, 1), f32)
    for at, frm in ((0, 0), (16, RANK), (32, 0), (48, RANK + NS), (64, 0), (96, 0)):
        w_x[at:at + 16], b_x[at:at + 16, 0] = wx[frm:frm + 16], bx[frm:frm + 16]
    w_dt = _np.zeros((P, DI), f32)
    for at in (0, 32, 64, 96):
        w_dt[at:at + RANK] = x["L0_attn_W_dt"].T
    bcat = x["L0_ffn_B"].transpose(0, 2, 1).reshape(NE * LR, FF)
    lora = _np.zeros((P, 2, FF), f32)
    for choice in range(2):
        for at in range(0, 64, 16):
            lora[64 * choice + at:64 * choice + at + 16, choice] = bcat
    w_ga = _np.concatenate([x["L0_ffn_Wg"], x["L0_ffn_A"].reshape(NE * LR, D)], 0).T
    a_log = x["L0_attn_A_log"].reshape(M, J, 32, KG, 4).transpose(4, 2, 0, 3, 1).reshape(P, UNITS)
    tri = _np.broadcast_to(_np.tril(_np.ones((NE, NE), f32), -1), (P, TT, NE, NE))
    arrays = dict(
        u=u, w_in=blocks(x["L0_attn_W_in"].T), b_in=x["L0_attn_b_in"].reshape(-1, P).T, w_x=blocks(w_x.T), b_x=b_x,
        w_dt=w_dt, b_dt=x["L0_attn_b_dt"].reshape(-1, P).T, a_log=a_log, d_skip=x["L0_attn_D"].reshape(-1, P).T,
        w_out=blocks(x["L0_attn_W_out"].T), b_out=_np.broadcast_to(x["L0_attn_b_out"], (P, D)), w_ga=blocks(w_ga),
        b_g=_np.broadcast_to(x["L0_ffn_bg"], (P, TT, NE)), w_i=blocks(x["L0_ffn_Wi"].T), w_o=blocks(x["L0_ffn_Wo"].T),
        lora_b=lora, ident_in=_np.eye(P, dtype=f32), nsum_in=_np.tile(_np.eye(32, dtype=f32), (4, 1)), tri_in=tri)
    nc = _bacc.Bacc("TRN2", target_bir_lowering=False, num_devices=1, dynamic_dma_scratch_size=2048)
    ins, args = {}, {}
    for name, a in arrays.items():
        ins[f"in_{name}"] = _np.ascontiguousarray(a)
        args[name] = nc.dram_tensor(f"in_{name}", a.shape, _mybir.dt.from_np(a.dtype), kind="ExternalInput").ap()
    out = nc.dram_tensor("out_x", (NC, T, D), _mybir.dt.from_np(_np.dtype(f32)), kind="ExternalOutput").ap()
    block_program(nc, out=out, **args)
    r = _run(nc, [ins], core_ids=[0])
    got = r.results[0]["out_x"]
    return got.reshape(SEQ // T, BATCH, T, D).transpose(1, 0, 2, 3).reshape(BATCH, SEQ, D)
```

```python
from contextlib import ExitStack

import numpy as np
import concourse.bass as bass
from concourse import mybir

F32 = mybir.dt.float32
F32R = mybir.dt.float32r
ALU = mybir.AluOpType
ACT = mybir.ActivationFunctionType
AX = mybir.AxisListType.X

P = 128
BATCH, SEQ, D = 4, 2048, 256
DI, NS, RANK = 512, 16, 16
FF, NE, LR = 1024, 4, 4
T = 512
NC = BATCH * SEQ // T
TT = T // P
KD = D // P
M = DI // P
J = P // 32
KG = NS // 4
STEPS = M * KG
UNITS = STEPS * J
NF = FF // P
NP = 2 * TT
EPS = 1e-5
BIG = 1e18

PE_SIDE = [
    "K1 late, S5 late, J6 late, T4 late | T5 late",
    "S6 late, J7 late | ",
    "A0 pre, A1 pre, K2 late | S7 late",
    "B0 pre, E0 main | F0 post, T6 late",
    "F1 post, B1 pre | B2 pre",
    "F2 post, F3 post | T7 late",
    "B3 pre | ",
    "C0 pre | G0 post, E1 main",
    "G1 post, D0 pre | D1 pre, H0 post",
    " | K3 late, E2 main",
    "I0 post | J0 post",
    "J1 post, S0 post | T0 post",
    "S1 post, J2 post | S2 post",
    "T1 post, J3 post, K0 post | S3 post, E3 main, T2 post",
    "J4 post | D2 pre, S4 post, T3 post",
    "J5 post, D3 pre | ",
]
ACT_SIDE = [
    "L1 main, M1 main | S5 late | T4 late | J6 late",
    "R1 pre |  | O0 pre, O1 pre, O2 pre, O3 pre | T5 late, S6 late",
    "J7 late |  | A0 pre, A1 pre | ",
    "S7 late | E0 main | B0 pre | ",
    " | T6 late |  | ",
    "B1 pre | B2 pre |  | Z0 main",
    " |  |  | R2 post",
    "B3 pre | Q0 post, Q1 post, Q2 post, Q3 post |  | C0 pre",
    "G0 post | G1 post, E1 main |  | ",
    "T7 late, D0 pre |  | D1 pre | L0 pre",
    "Z1 main | X0 post | E2 main, M0 pre | I0 post",
    " | J0 post |  | S0 post, J1 post",
    " |  | S1 post | J2 post",
    "T0 post | S2 post | T1 post | J3 post, Z2 main, S3 post, E3 main",
    "T2 post |  | J4 post | S4 post",
    "T3 post, D2 pre | D3 pre |  | J5 post, Z3 main",
]
DVE_SIDE = [
    "N0 pre |  | K1 late | O0 pre",
    " |  | Y3 post | ",
    " |  |  | ",
    " | W0 main | F0 post, K2 late | ",
    " |  |  | ",
    "F1 post |  |  | F2 post, F3 post, Y0 main",
    " | P0 post |  | Q0 post",
    " |  |  | ",
    "C0 pre |  |  | ",
    "W1 main | H0 post |  | ",
    "H1 post | Y1 main | K3 late | ",
    " |  |  | ",
    " |  | W2 main | ",
    " | Y2 main |  | ",
    "K0 post |  |  | W3 main",
    " |  |  | ",
]
POOL_SIDE = [
    "S3 post, R4 late, R5 late",
    "",
    "G3 post, V1 main",
    "U1 main, R6 late",
    "S0 main",
    "R7 late",
    "",
    "G0 main",
    "",
    "S1 main",
    "V0 pre, G1 main",
    "R0 post",
    "U0 pre, S2 main",
    "G2 main, R1 post, R2 post",
    "R3 post",
    "",
]
SP_SIDE = [
    "",
    "",
    "",
    "K1 late",
    "",
    "",
    "",
    "",
    "K2 late",
    "",
    "",
    "K3 late",
    "",
    "",
    "",
    "K0 post",
]
DECAYS = 3
BANKS = 4
BANK_JOBS = "ABCDEFGHIJTK"
PHASE = {"pre": 0, "main": 1, "post": 2, "late": 3}


def split_table(table):
    rows = [[[x.strip() for x in part.split(",") if x.strip()] for part in row.split("|")] for row in table]
    return [row + [[]] * (J - len(row)) for row in rows]


SIDE = {"pe": split_table(PE_SIDE), "act": split_table(ACT_SIDE), "dve": split_table(DVE_SIDE),
        "pool": split_table(POOL_SIDE), "sp": split_table(SP_SIDE)}


def bank_jobs():
    return [x for row in SIDE["pe"] for part in row for x in part if x[0] in BANK_JOBS]


def place(engine, letter, i):
    for s, row in enumerate(SIDE[engine]):
        for j, part in enumerate(row):
            for x in part:
                if x.startswith(f"{letter}{i}"):
                    return J * s + j + UNITS * PHASE[x.split()[1]]


def assign_banks():
    free = [0] * BANKS
    for _ in range(2):
        free, bank = [x - UNITS for x in free], {}
        for x in bank_jobs():
            bank[x] = free.index(min(free))
            letter, i = x[0], int(x[1])
            reader = {"F": "F", "K": "K", "H": "H"}.get(letter)
            at = place("dve", letter, i) if reader else place("act", "S" if letter == "J" else letter, i)
            free[bank[x]] = at - UNITS * PHASE[x.split()[1]]
    return bank


def parts_of(c):
    got = set()
    if 0 <= c < NC:
        got.add("main")
    if c + 1 < NC:
        got.add("pre")
    if 0 <= c - 1 < NC:
        got.add("post")
    if 0 <= c - 2 < NC:
        got.add("late")
    return got


BANK = assign_banks()


def used(job, c, off=0):
    def count(at):
        n = 0
        for body in range(-1, at + 1):
            for x in bank_jobs():
                if x.split()[1] in parts_of(body) and BANK[x] == BANK[job]:
                    n += 1
                if body == at and x == job:
                    break
        return n

    if isinstance(c, int):
        return count(c + off)
    first, slope = count(2 + off), count(3 + off) - count(2 + off)
    assert all(count(x + off) == first + (x - 2) * slope for x in range(2, NC - 2))
    return c * slope + (first - 2 * slope)


def block_program(nc, u, w_in, b_in, w_x, b_x, w_dt, b_dt, a_log, d_skip, w_out, b_out, w_ga, b_g, w_i, w_o,
                  lora_b, ident_in, nsum_in, tri_in, out):
    with ExitStack() as ctx:
        def sb(name, shape, dt=F32):
            return ctx.enter_context(nc.sbuf_tensor(name, shape, dt))

        def sem(name):
            return ctx.enter_context(nc.semaphore(name))

        bc_dram = nc.dram_tensor("bc_scratch", (2, NS, T), F32, kind="Internal").ap()
        rep_dram = nc.dram_tensor("rep_scratch", (2, M, P, T), F32, kind="Internal").ap()

        w_in_sb = sb("w_in_sb", [P, KD, 2 * DI])
        w_x_sb = sb("w_x_sb", [P, M, P])
        w_dt_st = sb("w_dt_st", [P, DI], F32R)
        w_out_sb = sb("w_out_sb", [P, M, D])
        w_ga_sb = sb("w_ga_sb", [P, KD, NE + NE * LR])
        w_i_sb = sb("w_i_sb", [P, KD, FF])
        w_o_sb = sb("w_o_sb", [P, NF, D])
        lora_st = sb("lora_st", [P, 2, FF], F32R)
        ident = sb("ident", [P, P])
        nsum = sb("nsum", [P, 32])
        tri = sb("tri", [P, TT, NE, NE])
        b_in_sb = sb("b_in_sb", [P, 2 * M])
        nb_z = sb("nb_z", [P, M])
        b_x_sb = sb("b_x_sb", [P, 1])
        b_dt_sb = sb("b_dt_sb", [P, M])
        d_sb = sb("d_sb", [P, M])
        a_sb = sb("a_sb", [P, UNITS])
        b_out_st = sb("b_out_st", [P, D], F32R)
        ones = sb("ones", [P, P], F32R)
        b_g_sb = sb("b_g_sb", [P, TT, NE])
        xin = sb("xin", [P, TT, D])
        xn_t = [sb(f"xn_t{i}", [P, KD, T]) for i in range(2)]
        x_t = [sb(f"x_t{i}", [P, M, T]) for i in range(2)]
        dbc = sb("dbc", [P, T])
        dt_st = sb("dt_st", [P, T], F32R)
        z_dt = sb("z_dt", [P, 2, T])
        e_dt = sb("e_dt", [P, 2, T])
        z_gate = [sb(f"z_gate{i}", [P, T]) for i in range(2)]
        e_gate = sb("e_gate", [P, T])
        gated = [sb(f"gated{i}", [P, M, T]) for i in range(2)]
        b_rep = sb("b_rep", [P, KG, T])
        c_rep = sb("c_rep", [P, KG, T])
        dt_rep = [sb(f"dt_rep{i}", [P, J, T]) for i in range(2)]
        dx_rep = [sb(f"dx_rep{i}", [P, J, T]) for i in range(2)]
        hs = [sb(f"hs{i}", [P, J, T]) for i in range(4)]
        state = [sb(f"state{i}", [P, UNITS]) for i in range(2)]
        state_next = [sb(f"state_next{i}", [P, UNITS]) for i in range(2)]
        xr = sb("xr", [P, TT, D])
        x1 = [sb(f"x1_{i}", [P, TT, D]) for i in range(2)]
        x2_t = sb("x2_t", [P, KD, T])
        low_t = sb("low_t", [P, T], F32R)
        r1 = [sb(f"r1_{i}", [P, T]) for i in range(2)]
        r2 = [sb(f"r2_{i}", [P, T]) for i in range(2)]
        r_t = sb("r_t", [P, NF, P])
        st1 = sb("st1", [P, TT, 6])
        mv1 = sb("mv1", [P, TT, 2])
        ve1 = sb("ve1", [P, TT])
        rs1 = sb("rs1", [P, TT])
        nt1 = sb("nt1", [P, TT])
        st2 = sb("st2", [P, TT, 6])
        mv2 = sb("mv2", [P, TT, 2])
        ve2 = sb("ve2", [P, TT])
        rs2 = sb("rs2", [P, TT])
        nt2 = sb("nt2", [P, TT])
        lg = sb("lg", [P, TT, NE])
        low = sb("low", [P, TT, NE * LR])
        mx = sb("mx", [P, TT])
        lm = sb("lm", [P, TT, NE])
        pexp = sb("pexp", [P, TT, NE])
        sm = sb("sm", [P, TT])
        rsm = sb("rsm", [P, TT])
        sc = sb("sc", [P, TT, NE])
        gt = sb("gt", [P, TT, NE, NE])
        eq = sb("eq", [P, TT, NE, NE])
        rank = sb("rank", [P, TT, NE])
        sel = sb("sel", [P, 2, TT, NE])
        wk = sb("wk", [P, 2, TT, NE])
        wgt = sb("wgt", [P, 2, TT])
        msk = sb("msk", [P, 2, TT, NE, LR])
        msk_hi = sb("msk_hi", [P, 2, TT, NE * LR], F32R)
        pk = sb("pk", [P, TT, 2, 2, 2, NE * LR])

        decay = [ctx.enter_context(nc.psum_tensor(f"decay{i}", [P, T], F32)) for i in range(DECAYS)]
        y_ps = ctx.enter_context(nc.psum_tensor("y_ps", [P, T], F32))
        banks = [ctx.enter_context(nc.psum_tensor(f"bank{i}", [P, 512], F32)) for i in range(BANKS)]
        filled = [sem(f"filled{i}") for i in range(BANKS)]
        freed = [sem(f"freed{i}") for i in range(BANKS)]

        (w_first, w_later, zeroed, a_ready, raw_rounded, weights_split, xin_loaded, ln1_part, ln1_root, ln1_newton, xn_ready,
         dt_hi, dt_lo, exp_dt, log_dt, delta_ready, dx_ready, bc_stored, rep_stored) = (sem(n) for n in (
            "w_first", "w_later", "zeroed", "a_ready", "raw_rounded", "weights_split", "xin_loaded", "ln1_part", "ln1_root",
            "ln1_newton", "xn_ready", "dt_hi", "dt_lo", "exp_dt", "log_dt", "delta_ready", "dx_ready",
            "bc_stored", "rep_stored"))
        rep_loaded = [sem(f"rep_loaded{i}") for i in range(2)]
        b_loaded = [sem(f"b_loaded{k}") for k in range(KG)]
        c_loaded = [sem(f"c_loaded{k}") for k in range(KG)]
        (decay_ready, input_ready, scan_done, state_moved, state_kept, prod_ready, nsum_done, y_read, gated_ready,
         clamp_z, log_z, sig_ready, silu_ready) = (sem(n) for n in (
            "decay_ready", "input_ready", "scan_done", "state_moved", "state_kept", "prod_ready", "nsum_done", "y_read",
            "gated_ready", "clamp_z", "log_z", "sig_ready", "silu_ready"))
        (xr_loaded, ln2_part, ln2_root, ln2_newton, x2_ready, router, router_exp, masks_ready, r1_ready,
         z2_ready) = (sem(n) for n in (
            "xr_loaded", "ln2_part", "ln2_root", "ln2_newton", "x2_ready", "router", "router_exp",
            "masks_ready", "r1_ready", "z2_ready"))
        sp_turn, last_sums = sem("sp_turn"), sem("last_sums")
        router_step, mask_split = sem("router_step"), sem("mask_split")
        R_STEPS = 13
        out_stored = [sem(f"out_stored{t}") for t in range(TT)]

        block = ctx.enter_context(nc.Block())

        def at_least(eng, s, value):
            if not (isinstance(value, int) and value <= 0):
                eng.wait_ge(s, value)

        def chunk_of(c, when):
            return c + {"pre": 1, "main": 0, "post": -1, "late": -2}[when]

        def is_last(q):
            return isinstance(q, int) and q == NC - 1

        def odd_of(par, when):
            return (par + {"pre": 1, "main": 0, "post": 1, "late": 0}[when]) % 2

        def wait_filled(eng, job, c):
            eng.wait_ge(filled[BANK[job]], used(job, c))
            return banks[BANK[job]], freed[BANK[job]]

        def wait_read(eng, c, when, letter, numbers, own=None):
            last = {}
            for place_, job in enumerate(bank_jobs()):
                if job[0] == letter and int(job[1]) in numbers:
                    off = PHASE[job.split()[1]] - PHASE[when]
                    last[BANK[job]] = max(last.get(BANK[job], (-9, 0, "")), (off, place_, job))
            for b, (off, _, job) in last.items():
                if b != own:
                    eng.wait_ge(freed[b], used(job, c, off))

        def sweep(eng, body):
            for c in (-1, 0, 1):
                body(c, c % 2, parts_of(c))
            with eng.Fori(1, (NC - 2) // 2) as pair:
                for odd in range(2):
                    body(pair * 2 + odd, odd, parts_of(2))
            for c in (NC - 2, NC - 1, NC, NC + 1):
                body(c, c % 2, parts_of(c))

        def side(engine, s, j, parts):
            for job in SIDE[engine][s][j]:
                if job.split()[1] in parts:
                    yield job[0], int(job[1]), job.split()[1], job

        raw_lora = hs[2][:].rearrange("p a t -> p (a t)").rearrange("p (a t) -> p a t", a=2)
        raw_b_out = hs[3][:, 0, 0:D]
        first_loads = ((w_in_sb[:], w_in), (ident[:], ident_in), (b_in_sb[:], b_in), (nb_z[:], b_in[:, M:2 * M]),
                       (w_x_sb[:], w_x), (b_x_sb[:], b_x), (hs[1][:, 0, :], w_dt), (b_dt_sb[:], b_dt),
                       (a_sb[:], a_log), (d_sb[:], d_skip), (nsum[:], nsum_in))
        later_loads = ((raw_lora, lora_b), (w_out_sb[:], w_out), (w_ga_sb[:], w_ga), (tri[:], tri_in),
                       (b_g_sb[:], b_g), (raw_b_out, b_out), (w_i_sb[:], w_i), (w_o_sb[:], w_o))

        def wait_first(eng):
            eng.wait_ge(w_first, 16 * len(first_loads))

        def wait_later(eng):
            eng.wait_ge(w_later, 16 * len(later_loads))

        @block.sync
        def _(sp):
            sp.dma_start(xin[:], u[0].rearrange("(t p) d -> p t d", p=P)).then_inc(xin_loaded, 16)
            for dst, src in first_loads:
                sp.dma_start(dst, src).then_inc(w_first, 16)
            for dst, src in later_loads:
                sp.dma_start(dst, src).then_inc(w_later, 16)

            def load_rep(c, m):
                for kind, dst in enumerate((dt_rep, dx_rep)):
                    for n in range(4):
                        sp.dma_start(dst[m % 2][32 * n:32 * n + 32, :, :],
                                     rep_dram[kind, m].rearrange("(j d) t -> d j t", j=J)).then_inc(rep_loaded[m % 2], 16)

            def load_bc(which, k):
                dst, s = ((b_rep, b_loaded), (c_rep, c_loaded))[which]
                for n in range(4):
                    sp.dma_start(dst[32 * n:32 * n + 32, k, :],
                                 bc_dram[which, 4 * k + n:4 * k + n + 1, :].to_broadcast([32, T])).then_inc(s[k], 16)

            def waits(*needs):
                for s_, at in needs:
                    at_least(sp, s_, at)
                    if not isinstance(at, int):
                        sp.sem_inc(sp_turn, 1)

            def filled_by(job, c):
                return filled[BANK[job]], used(job, c)

            def read_by(job, c):
                return freed[BANK[job]], used(job, c)

            def store_rep(c, pair):
                back = [(rep_loaded[i], 256 * c - (128 if pair == 0 else 0)) for i in range(2)]
                waits(*back, (delta_ready, 2 * c + pair + 1), (dx_ready, 2 * c + pair + 1))
                for kind, src in enumerate((e_dt, z_dt)):
                    sp.dma_start(rep_dram[kind, 2 * pair:2 * pair + 2].rearrange("m p t -> p m t"),
                                 src[:]).then_inc(rep_stored, 16)

            def chunk_rows(dram, c):
                return dram[bass.ds(c, 1)]

            def store_out(t, when, job, c, par):
                dst = chunk_rows(out, chunk_of(c, when))
                waits(read_by(job, c))
                sp.dma_start(dst[:, t * P:(t + 1) * P, :].rearrange("o p d -> p (o d)"),
                             x1[odd_of(par, when)][:, t, :]).then_inc(out_stored[t], 16)

            def body(c, par, parts):
                def past(m):
                    return (decay_ready, UNITS * c + KG * J * m), (input_ready, 2 * (STEPS * c + KG * m))

                for s in range(STEPS):
                    m, k = divmod(s, KG)
                    if "main" in parts and s == 0:
                        waits((prod_ready, STEPS * c))
                        load_bc(1, KG - 1)
                    if "main" in parts and k == 1 and m + 1 < M:
                        waits(*past(m), (rep_stored, 64 * c + 32 * (2 if m >= 1 else 1)))
                        load_rep(c, m + 1)
                    if "pre" in parts and s == 2 and (not isinstance(c, int) or c + 2 < NC):
                        src = chunk_rows(u, c + 2)
                        waits(filled_by("A1 pre", c))
                        sp.dma_start(xin[:], src.rearrange("o (t p) d -> p (o t) d", p=P)).then_inc(xin_loaded, 16)
                    if "main" in parts and s == 4:
                        store_rep(c, 1)
                    for _, t, when, job in side("sp", s, 0, parts):
                        store_out(t, when, job, c, par)
                    if "pre" in parts and s == 8:
                        back = [(x[kk], 64 * (c + 1)) for kk in range(KG) for x in (b_loaded, c_loaded)]
                        waits(read_by("C0 pre", c), *back)
                        sp.dma_start(bc_dram[0], dbc[16:32, :]).then_inc(bc_stored, 16)
                        sp.dma_start(bc_dram[1], dbc[48:64, :]).then_inc(bc_stored, 16)
                    if "main" in parts and s == 11:
                        src = chunk_rows(u, c)
                        if "post" in parts:
                            waits(filled_by("G1 post", c))
                        sp.dma_start(xr[:], src.rearrange("o (t p) d -> p (o t) d", p=P)).then_inc(xr_loaded, 16)
                    if "pre" in parts and s == 13:
                        store_rep(c + 1, 0)
                        waits((rep_stored, 64 * (c + 1) + 32), *past(M - 1))
                        load_rep(c + 1, 0)
                    if "pre" in parts and s >= 12:
                        if s == 12:
                            waits((bc_stored, 32 * (c + 2)))
                        waits((input_ready, 2 * (STEPS * c + s + 1)))
                        load_bc(0, s - 12)
                        if s > 12:
                            waits((prod_ready, STEPS * c + s))
                            load_bc(1, s - 13)

            sweep(sp, body)
            for t in range(TT):
                sp.wait_ge(out_stored[t], 16 * NC)

        @block.tensor
        def _(pe):
            wait_first(pe)

            def job_pe(letter, i, when, job, c, par):
                q, odd = chunk_of(c, when), odd_of(par, when)
                if letter == "S":
                    t, half = divmod(i, 2)
                    tile = next(x for x in bank_jobs() if x.startswith(f"J{i}"))
                    pe.wait_ge(r1_ready, NP * q + i + 1)
                    pe.matmul(banks[BANK[tile]][:], low_t[:, t * P:(t + 1) * P],
                              lora_st[:, 1, half * 512:(half + 1) * 512],
                              start=False, stop=True, skip_group_check=True).then_inc(z2_ready, 1)
                    return
                b = BANK[job]
                ps = banks[b]
                at_least(pe, freed[b], used(job, c) - 1)

                def needs(other, *numbers):
                    wait_read(pe, c, when, other, numbers, own=b)

                if letter in "AG":
                    pe.wait_ge(xn_ready if letter == "A" else x2_ready, TT * (q + 1))
                    src = xin if letter == "A" else xr
                    for t in range(TT):
                        mm = pe.transpose(ps[:, t * P:(t + 1) * P], src[:, t, i * P:(i + 1) * P], ident[:])
                elif letter in "BE":
                    if letter == "B":
                        needs("A", 0, 1)
                    col = i * P + (DI if letter == "E" else 0)
                    for k in range(KD):
                        mm = pe.matmul(ps[:], w_in_sb[:, k, col:col + P], xn_t[odd][:, k, :], start=k == 0, stop=k == KD - 1)
                elif letter == "C":
                    for k in range(M):
                        needs("B", k)
                        mm = pe.matmul(ps[:], w_x_sb[:, k, :], x_t[odd][:, k, :], start=k == 0, stop=k == M - 1)
                elif letter == "D":
                    if isinstance(c, int) and c < 0:
                        pe.wait_ge(weights_split, 1)
                    pe.wait_ge(dt_lo, q + 1)
                    mm = pe.matmul(ps[:], w_dt_st[:, i * P:(i + 1) * P], dt_st[:], start=True, stop=True)
                elif letter == "F":
                    pe.wait_ge(gated_ready, M * (q + 1))
                    for k in range(M):
                        pe.matmul(ps[:, 0:D], gated[odd][:, k, i * P:(i + 1) * P], w_out_sb[:, k, :], start=k == 0, stop=False)
                    mm = pe.matmul(ps[:, 0:D], ones[:], b_out_st[:], start=False, stop=True)
                elif letter == "H":
                    w = NE + NE * LR
                    needs("G", 0, 1)
                    for t in range(TT):
                        for k in range(KD):
                            mm = pe.matmul(ps[:, t * w:(t + 1) * w], x2_t[:, k, t * P:(t + 1) * P], w_ga_sb[:, k, :],
                                           start=k == 0, stop=k == KD - 1)
                elif letter == "I":
                    pe.wait_ge(masks_ready, q + 1)
                    for t in range(TT):
                        mm = pe.transpose(ps[:, t * P:(t + 1) * P], pk[:, t].rearrange("p a b c d -> p (a b c d)"), ident[:])
                elif letter == "J":
                    t, half = divmod(i, 2)
                    cols = slice(half * 512, (half + 1) * 512)
                    if i == 0:
                        needs("I", 0)
                    for k in range(KD):
                        pe.matmul(ps[:], x2_t[:, k, t * P:(t + 1) * P], w_i_sb[:, k, cols], start=k == 0, stop=False)
                    mm = pe.matmul(ps[:], low_t[:, t * P:(t + 1) * P], lora_st[:, 0, cols], start=False, stop=True)
                elif letter == "T":
                    if is_last(q):
                        pe.wait_ge(last_sums, i + 1)
                        for f in range(4):
                            mm = pe.transpose(ps[:, f * P:(f + 1) * P], r1[i % 2][:, f * P:(f + 1) * P], ident[:])
                    else:
                        wait_read(pe, c, when, "J", [i], own=b)
                        for f in range(4):
                            for r in (r1, r2):
                                mm = pe.matmul(ps[:, f * P:(f + 1) * P], r[i % 2][:, f * P:(f + 1) * P], ident[:],
                                               start=r is r1, stop=r is r2)
                elif letter == "K":
                    needs("T", 2 * i, 2 * i + 1)
                    for f in range(NF):
                        mm = pe.matmul(ps[:, 0:D], r_t[:, f, :], w_o_sb[:, f, :], start=f == 0, stop=f == NF - 1)
                mm.then_inc(filled[b], 1)

            def sum_states(c, s):
                m, k = divmod(s, KG)
                pe.wait_ge(prod_ready, STEPS * c + s + 1)
                if k == 0:
                    at_least(pe, y_read, M * c + m)
                for j in range(J):
                    mm = pe.matmul(y_ps[32 * j:32 * j + 32, :], nsum[:], hs[s % 4][:, j, :], start=k == 0,
                                   stop=k == KG - 1)
                mm.then_inc(nsum_done, 1)

            def body(c, par, parts):
                if isinstance(c, int) and c == 0:
                    wait_later(pe)
                    pe.wait_ge(weights_split, 3)
                for s in range(STEPS):
                    for job in side("pe", s, 0, parts):
                        job_pe(*job, c, par)
                    if s >= 2 and "main" in parts:
                        sum_states(c, s - 2)
                    if s < 2 and "post" in parts:
                        sum_states(c - 1, STEPS - 2 + s)
                    for job in side("pe", s, 1, parts):
                        job_pe(*job, c, par)

            sweep(pe, body)

        @block.scalar
        def _(act):
            nc.scalar.preload_act_table_set("natural_log_exp_and_others")
            wait_first(act)
            nc.scalar.activation(a_sb[:], a_sb[:], ACT.Exp).then_inc(a_ready, 1)
            act.wait_ge(a_ready, 1)
            nc.scalar.mul(a_sb[:], a_sb[:], -1.0).then_inc(a_ready, 1)
            nc.scalar.mul(nb_z[:], nb_z[:], -1.0).then_inc(a_ready, 1)
            act.wait_ge(a_ready, 3)

            def job_act(letter, i, when, job, c, par):
                q, odd = chunk_of(c, when), odd_of(par, when)
                big = not isinstance(q, int)
                if letter == "A":
                    ps, free = wait_filled(act, job, c)
                    nc.scalar.copy(xn_t[odd][:, i, :], ps[:]).then_inc(free, 1)
                elif letter == "B":
                    at_least(act, y_read, M * (q - 2) + i + 1 if big or q >= 2 else 0)
                    at_least(act, dx_ready, 2 * (q - 1) if big or q >= 2 else 0)
                    ps, free = wait_filled(act, job, c)
                    nc.scalar.activation(x_t[odd][:, i, :], ps[:], ACT.Identity, bias=b_in_sb[:, i:i + 1]).then_inc(free, 1)
                elif letter == "C":
                    at_least(act, bc_stored, 32 * q)
                    at_least(act, dt_lo, q)
                    ps, free = wait_filled(act, job, c)
                    nc.scalar.activation(dbc[:], ps[:], ACT.Identity, bias=b_x_sb[:, 0:1]).then_inc(free, 1)
                    wait_read(act, c, when, "C", [0])
                    nc.scalar.activation(dt_st[:], dbc[:], ACT.Identity).then_inc(dt_hi, 1)
                elif letter == "D":
                    if i % 2 == 0:
                        at_least(act, rep_stored, 64 * q + 32 * (i // 2))
                    ps, free = wait_filled(act, job, c)
                    nc.scalar.activation(z_dt[:, i % 2, :], ps[:], ACT.Relu, bias=b_dt_sb[:, i:i + 1])
                    nc.scalar.activation(e_dt[:, i % 2, :], ps[:], ACT.Abs, bias=b_dt_sb[:, i:i + 1]).then_inc(free, 1)
                elif letter == "L":
                    wait_read(act, c, when, "D", (2 * i, 2 * i + 1))
                    nc.scalar.activation(e_dt[:], e_dt[:], ACT.Exp, scale=-1.0).then_inc(exp_dt, 1)
                elif letter == "M":
                    act.wait_ge(exp_dt, 2 * q + i + 1)
                    nc.scalar.activation(e_dt[:], e_dt[:], ACT.Ln, bias=1.0).then_inc(log_dt, 1)
                elif letter == "E":
                    at_least(act, gated_ready, M * q + i - 1)
                    ps, free = wait_filled(act, job, c)
                    nc.scalar.activation(z_gate[i % 2][:], ps[:], ACT.Identity, bias=b_in_sb[:, M + i:M + i + 1])
                    at_least(act, silu_ready, M * q + i)
                    nc.scalar.activation(e_gate[:], ps[:], ACT.Exp, scale=-1.0, bias=nb_z[:, i:i + 1]).then_inc(free, 1)
                elif letter == "Z":
                    act.wait_ge(clamp_z, M * q + i + 1)
                    nc.scalar.activation(e_gate[:], e_gate[:], ACT.Ln).then_inc(log_z, 1)
                    act.wait_ge(log_z, M * q + i + 1)
                    nc.scalar.activation(e_gate[:], e_gate[:], ACT.Exp, scale=-1.0).then_inc(sig_ready, 1)
                elif letter == "R":
                    ve, rs, part, root = (ve1, rs1, ln1_part, ln1_root) if i == 1 else (ve2, rs2, ln2_part, ln2_root)
                    act.wait_ge(part, 3 * (q + 1))
                    nc.scalar.activation(rs[:], ve[:], ACT.Ln).then_inc(root, 1)
                    act.wait_ge(root, 2 * q + 1)
                    nc.scalar.activation(rs[:], rs[:], ACT.Exp, scale=-0.5).then_inc(root, 1)
                elif letter in "OQ":
                    src, dst, rs, nt, newton, done = ((xin, xin, rs1, nt1, ln1_newton, xn_ready) if letter == "O"
                                                      else (x1[odd], xr, rs2, nt2, ln2_newton, x2_ready))
                    act.wait_ge(newton, 5 * (q + 1))
                    nc.scalar.activation(dst[:, i, :], src[:, i, :], ACT.Identity, scale=rs[:, i:i + 1],
                                         bias=nt[:, i:i + 1]).then_inc(done, 1)
                elif letter == "G":
                    ps, free = wait_filled(act, job, c)
                    nc.scalar.copy(x2_t[:, i, :], ps[:]).then_inc(free, 1)
                elif letter == "X":
                    act.wait_ge(router, q + 1)
                    nc.scalar.activation(pexp[:], lm[:], ACT.Exp).then_inc(router_exp, 1)
                elif letter == "I":
                    ps, free = wait_filled(act, job, c)
                    nc.scalar.activation(low_t[:], ps[:], ACT.Identity).then_inc(free, 1)
                elif letter == "J":
                    before = next(x for x in bank_jobs() if x.startswith(f"T{(i - 2) % NP}"))
                    if i >= 2 or not isinstance(q, int) or q >= 1:
                        off = PHASE[before.split()[1]] - PHASE[when] - (i < 2)
                        if BANK[before] != BANK[job]:
                            act.wait_ge(filled[BANK[before]], used(before, c, off))
                    ps, _ = wait_filled(act, job, c)
                    nc.scalar.activation(r1[i % 2][:], ps[:], ACT.Relu, scale=wgt[:, 0, i // 2:i // 2 + 1]).then_inc(r1_ready, 1)
                elif letter == "S":
                    act.wait_ge(z2_ready, NP * q + i + 1)
                    b = BANK[next(x for x in bank_jobs() if x.startswith(f"J{i}"))]
                    nc.scalar.activation(r2[i % 2][:], banks[b][:], ACT.Relu,
                                         scale=wgt[:, 1, i // 2:i // 2 + 1]).then_inc(freed[b], 1)
                elif letter == "T":
                    ps, free = wait_filled(act, job, c)
                    nc.scalar.copy(r_t[:, 4 * (i % 2):4 * (i % 2) + 4, :].rearrange("p f t -> p (f t)"), ps[:]).then_inc(free, 1)

            def body(c, par, parts):
                for s in range(STEPS):
                    m, k = divmod(s, KG)
                    for j in range(J):
                        if "main" in parts:
                            n = UNITS * c + J * s + j
                            if j == 0 and k == 0:
                                act.wait_ge(rep_loaded[m % 2], 256 * c + 128 * (m // 2 + 1))
                            at_least(act, scan_done, n if s == j == 0 else n - DECAYS + 1)
                            nc.scalar.activation(decay[(J * s + j) % DECAYS][:], dt_rep[m % 2][:, j, :], ACT.Exp,
                                                 scale=a_sb[:, J * s + j:J * s + j + 1]).then_inc(decay_ready, 1)
                        if j in (1, 2) and s >= 1 and "main" in parts:
                            (move_state, keep_state)[j - 1](c, par, s - 1)
                        if j in (1, 2) and s == 0 and "post" in parts:
                            (move_state, keep_state)[j - 1](c - 1, 1 - par, STEPS - 1)
                        for job in side("act", s, j, parts):
                            job_act(*job, c, par)

            def move_state(c, par, s):
                cols = slice(J * s, J * s + J)
                act.wait_ge(scan_done, UNITS * c + J * (s + 1))
                nc.scalar.copy(state[par][:, cols], state_next[par][:, cols]).then_inc(state_moved, 1)

            def keep_state(c, par, s):
                act.wait_ge(state_moved, STEPS * c + s + 1)
                nc.scalar.copy(state_next[par][:, J * s:J * s + J], hs[s % 4][:, :, T - 1]).then_inc(state_kept, 1)

            sweep(act, body)

        @block.vector
        def _(dve):
            v = nc.vector
            for par in range(2):
                v.memset(state[par][:], 0.0)
                v.memset(state_next[par][:], 0.0).then_inc(zeroed, 1)
            def split_weights(st, raw, done):
                v.tensor_copy(st[:], raw).then_inc(raw_rounded, 1)
                dve.wait_ge(raw_rounded, done)
                for lo in (32, 96):
                    last = v.tensor_tensor(st[lo:lo + 32], raw[lo:lo + 32], st[lo:lo + 32].bitcast(F32), ALU.subtract)
                last.then_inc(weights_split, 1)

            def stats(q, src, st, mv, ve, part):
                for t in range(TT):
                    last = v.bn_stats(st[:, t, :], src[:, t, :])
                last.then_inc(part, 1)
                dve.wait_ge(part, 3 * q + 1)
                v.memset(ve[:], EPS)
                for t in range(TT):
                    last = v.bn_aggr(mv[:, t, :], st[:, t, :])
                last.then_inc(part, 1)
                dve.wait_ge(part, 3 * q + 2)
                v.tensor_tensor(ve[:], mv[:, :, 1], ve[:], ALU.add).then_inc(part, 1)

            def deviations(q, mv, ve, rs, nt, root, newton):
                dve.wait_ge(root, 2 * (q + 1))
                v.tensor_tensor(nt[:], rs[:], rs[:], ALU.mult).then_inc(newton, 1)
                dve.wait_ge(newton, 5 * q + 1)
                v.tensor_tensor(nt[:], nt[:], ve[:], ALU.mult).then_inc(newton, 1)
                dve.wait_ge(newton, 5 * q + 2)
                v.tensor_scalar(nt[:], nt[:], -0.5, 1.5, ALU.mult, ALU.add).then_inc(newton, 1)
                dve.wait_ge(newton, 5 * q + 3)
                v.tensor_tensor(rs[:], rs[:], nt[:], ALU.mult).then_inc(newton, 1)
                dve.wait_ge(newton, 5 * q + 4)
                v.scalar_tensor_tensor(out=nt[:], in0=mv[:, :, 0], scalar=-1.0, in1=rs[:], op0=ALU.mult,
                                       op1=ALU.mult).then_inc(newton, 1)

            def job_dve(letter, i, when, job, c, par):
                q, odd = chunk_of(c, when), odd_of(par, when)
                if letter == "N":
                    dve.wait_ge(xin_loaded, 16 * (q + 1))
                    stats(q, xin, st1, mv1, ve1, ln1_part)
                elif letter == "O":
                    deviations(q, mv1, ve1, rs1, nt1, ln1_root, ln1_newton)
                elif letter == "P":
                    wait_read(dve, c, when, "F", range(TT))
                    stats(q, x1[odd], st2, mv2, ve2, ln2_part)
                elif letter == "Q":
                    deviations(q, mv2, ve2, rs2, nt2, ln2_root, ln2_newton)
                elif letter == "C":
                    dve.wait_ge(dt_hi, q + 1)
                    v.tensor_tensor(dt_st[64:128], dbc[64:128], dt_st[64:128].bitcast(F32), ALU.subtract).then_inc(dt_lo, 1)
                elif letter == "W":
                    wait_read(dve, c, when, "E", [i])
                    v.tensor_scalar(e_gate[:], e_gate[:], BIG, 1.0, ALU.min, ALU.add).then_inc(clamp_z, 1)
                elif letter == "Y":
                    dve.wait_ge(nsum_done, STEPS * q + KG * (i + 1))
                    v.scalar_tensor_tensor(out=gated[odd][:, i, :], in0=x_t[odd][:, i, :], scalar=d_sb[:, i:i + 1],
                                           in1=y_ps[:], op0=ALU.mult, op1=ALU.add).then_inc(y_read, 1)
                elif letter == "F":
                    if i == 0:
                        dve.wait_ge(xr_loaded, 16 * (q + 1))
                    at_least(dve, out_stored[i], 16 * (q - 1))
                    ps, free = wait_filled(dve, job, c)
                    v.tensor_tensor(x1[odd][:, i, :], ps[:, 0:D], xr[:, i, :], ALU.add).then_inc(free, 1)
                elif letter == "K":
                    ps, free = wait_filled(dve, job, c)
                    v.tensor_tensor(x1[odd][:, i, :], ps[:, 0:D], x1[odd][:, i, :], ALU.add).then_inc(free, 1)
                elif letter == "H" and i == 0:
                    ps, free = wait_filled(dve, job, c)
                    z = ps[:, 0:TT * (NE + NE * LR)].rearrange("p (t w) -> p t w", t=TT)
                    v.tensor_tensor(lg[:], z[:, :, 0:NE], b_g_sb[:], ALU.add).then_inc(router_step, 1)
                    v.tensor_copy(low[:], z[:, :, NE:]).then_inc(free, 1)
                    dve.wait_ge(router_step, R_STEPS * q + 1)
                    v.tensor_reduce(mx[:], lg[:], AX, ALU.max).then_inc(router_step, 1)
                    dve.wait_ge(router_step, R_STEPS * q + 2)
                    v.tensor_tensor(lm[:], lg[:], mx[:].unsqueeze(2).to_broadcast([P, TT, NE]), ALU.subtract).then_inc(router, 1)
                elif letter == "H":
                    choose(q)

            def choose(q):
                base = R_STEPS * q

                def then(n, ins):
                    ins.then_inc(router_step, 1)
                    dve.wait_ge(router_step, base + n)

                dve.wait_ge(router_exp, q + 1)
                then(3, v.tensor_reduce(sm[:], pexp[:], AX, ALU.add))
                then(4, v.reciprocal(rsm[:], sm[:]))
                then(5, v.tensor_tensor(sc[:], pexp[:], rsm[:].unsqueeze(2).to_broadcast([P, TT, NE]), ALU.mult))
                other = sc[:].unsqueeze(2).to_broadcast([P, TT, NE, NE])
                own = sc[:].unsqueeze(3).to_broadcast([P, TT, NE, NE])
                v.tensor_tensor(gt[:], other, own, ALU.is_gt)
                then(6, v.tensor_tensor(eq[:], other, own, ALU.is_equal))
                then(7, v.tensor_tensor(eq[:], eq[:], tri[:], ALU.mult))
                then(8, v.tensor_tensor(gt[:], gt[:], eq[:], ALU.add))
                then(9, v.tensor_reduce(rank[:], gt[:], AX, ALU.add))
                v.tensor_scalar(sel[:, 0], rank[:], 0.0, None, ALU.is_equal)
                then(10, v.tensor_scalar(sel[:, 1], rank[:], 1.0, None, ALU.is_equal))
                for a in range(2):
                    last = v.tensor_tensor(wk[:, a], sel[:, a], sc[:], ALU.mult)
                then(11, last)
                v.tensor_reduce(wgt[:], wk[:], AX, ALU.add)
                v.tensor_tensor(sel[:, 1], sel[:, 1], sel[:, 0], ALU.subtract).then_inc(router_step, 1)
                dve.wait_ge(router_step, base + 12)
                lw = low[:].rearrange("p t (e r) -> p t e r", e=NE)
                for a in range(2):
                    last = v.tensor_tensor(msk[:, a], lw, sel[:, a].unsqueeze(3).to_broadcast([P, TT, NE, LR]), ALU.mult)
                then(13, last)
                flat = msk[:].rearrange("p a t e r -> p a t (e r)")
                v.tensor_copy(msk_hi[:], flat).then_inc(mask_split, 1)
                dve.wait_ge(mask_split, q + 1)
                hi = msk_hi[:].bitcast(F32)
                for a in range(2):
                    for copy in range(2):
                        v.tensor_copy(pk[:, :, a, copy, 0], hi[:, a])
                        last = v.tensor_tensor(pk[:, :, a, copy, 1], flat[:, a], hi[:, a], ALU.subtract)
                last.then_inc(masks_ready, 1)

            def scan_input(c, par, s, half):
                m, k = divmod(s, KG)
                if half == 0:
                    if k == 0:
                        dve.wait_ge(rep_loaded[m % 2], 256 * c + 128 * (m // 2 + 1))
                    if m == 0:
                        dve.wait_ge(b_loaded[k], 64 * (c + 1))
                    at_least(dve, nsum_done, STEPS * c + s - 3)
                js = slice(2 * half, 2 * half + 2)
                v.tensor_tensor(hs[s % 4][:, js, :], dx_rep[m % 2][:, js, :],
                                b_rep[:, k, :].unsqueeze(1).to_broadcast([P, 2, T]), ALU.mult).then_inc(input_ready, 1)

            def body(c, par, parts):
                for s in range(STEPS):
                    if "main" not in parts and "pre" in parts and s == 2:
                        wait_first(dve)
                        split_weights(w_dt_st, hs[1][:, 0, :], 1)
                    for j in range(J):
                        if "main" in parts and j % 2 == 0:
                            if s + 1 < STEPS:
                                scan_input(c, par, s + 1, j // 2)
                            elif "pre" in parts:
                                scan_input(c + 1, 1 - par, 0, j // 2)
                            dve.wait_ge(input_ready, 2 * (STEPS * c + s) + j // 2 + 1)
                        if "main" in parts:
                            dve.wait_ge(decay_ready, UNITS * c + J * s + j + 1)
                            h = hs[s % 4][:, j, :]
                            v.tensor_tensor_scan(h, decay[(J * s + j) % DECAYS][:], h, state[par][:, J * s + j:J * s + j + 1],
                                                 ALU.mult, ALU.add).then_inc(scan_done, 1)
                        for job in side("dve", s, j, parts):
                            job_dve(*job, c, par)
                if "main" not in parts and "pre" in parts:
                    wait_later(dve)
                    v.tensor_scalar(ones[:], ident[:], 0.0, 1.0, ALU.mult, ALU.add)
                    split_weights(lora_st, raw_lora, 2)
                    split_weights(b_out_st, raw_b_out, 3)
                    dve.wait_ge(weights_split, 3)
                    for half in range(2):
                        scan_input(0, 0, 0, half)

            sweep(dve, body)

        @block.gpsimd
        def _(pool):
            wait_later(pool)

            def job_pool(letter, i, when, job, c, par):
                q, odd = chunk_of(c, when), odd_of(par, when)
                g = nc.gpsimd
                if letter == "U":
                    pool.wait_ge(delta_ready, 2 * q + i + 1)
                    g.tensor_tensor(z_dt[:], e_dt[:], x_t[odd][:, 2 * i:2 * i + 2, :], ALU.mult).then_inc(dx_ready, 1)
                elif letter == "S":
                    pool.wait_ge(sig_ready, M * q + i + 1)
                    g.tensor_tensor(z_gate[i % 2][:], z_gate[i % 2][:], e_gate[:], ALU.mult).then_inc(silu_ready, 1)
                elif letter == "G":
                    pool.wait_ge(y_read, M * q + i + 1)
                    pool.wait_ge(silu_ready, M * q + i + 1)
                    g.tensor_tensor(gated[odd][:, i, :], gated[odd][:, i, :], z_gate[i % 2][:], ALU.mult).then_inc(gated_ready, 1)
                elif letter == "R" and is_last(q):
                    wait_read(pool, c, when, "J", [i])
                    g.tensor_tensor(r1[i % 2][:], r1[i % 2][:], r2[i % 2][:], ALU.add).then_inc(last_sums, 1)
                elif letter == "V":
                    pool.wait_ge(log_dt, 2 * q + i + 1)
                    g.tensor_tensor(e_dt[:], e_dt[:], z_dt[:], ALU.add).then_inc(delta_ready, 1)

            def times_c(c, s):
                k = s % KG
                pool.wait_ge(scan_done, UNITS * c + J * (s + 1))
                pool.wait_ge(state_kept, STEPS * c + s + 1)
                if s < KG:
                    pool.wait_ge(c_loaded[k], 64 * (c + 1))
                nc.gpsimd.tensor_tensor(hs[s % 4][:], hs[s % 4][:], c_rep[:, k, :].unsqueeze(1).to_broadcast([P, J, T]),
                                        ALU.mult).then_inc(prod_ready, 1)

            def body(c, par, parts):
                for s in range(STEPS):
                    if s >= 1 and "main" in parts:
                        times_c(c, s - 1)
                    if s == 0 and "post" in parts:
                        times_c(c - 1, STEPS - 1)
                    for job in side("pool", s, 0, parts):
                        job_pool(*job, c, par)

            sweep(pool, body)


def kernel(**inputs):
    import numpy as _np
    import concourse.bacc as _bacc
    from concourse import mybir as _mybir
    from concourse.bass_utils import run_bass_kernel_spmd as _run

    x = {k: _np.asarray(a) for k, a in inputs.items()}
    f32 = _np.float32

    def blocks(a):
        return a.reshape(-1, P, a.shape[-1]).transpose(1, 0, 2)

    u = x["L0_attn_u"].reshape(BATCH, SEQ // T, T, D).transpose(1, 0, 2, 3).reshape(NC, T, D)
    wx, bx = x["L0_attn_W_x"], x["L0_attn_b_x"]
    w_x, b_x = _np.zeros((P, DI), f32), _np.zeros((P, 1), f32)
    for at, frm in ((0, 0), (16, RANK), (32, 0), (48, RANK + NS), (64, 0), (96, 0)):
        w_x[at:at + 16], b_x[at:at + 16, 0] = wx[frm:frm + 16], bx[frm:frm + 16]
    w_dt = _np.zeros((P, DI), f32)
    for at in (0, 32, 64, 96):
        w_dt[at:at + RANK] = x["L0_attn_W_dt"].T
    b_out = _np.zeros((P, D), f32)
    b_out[0] = b_out[32] = x["L0_attn_b_out"]
    bcat = x["L0_ffn_B"].transpose(0, 2, 1).reshape(NE * LR, FF)
    lora = _np.zeros((P, 2, FF), f32)
    for choice in range(2):
        for at in range(0, 64, 16):
            lora[64 * choice + at:64 * choice + at + 16, choice] = bcat
    w_ga = _np.concatenate([x["L0_ffn_Wg"], x["L0_ffn_A"].reshape(NE * LR, D)], 0).T
    a_log = x["L0_attn_A_log"].reshape(M, J, 32, KG, 4).transpose(4, 2, 0, 3, 1).reshape(P, UNITS)
    tri = _np.broadcast_to(_np.tril(_np.ones((NE, NE), f32), -1), (P, TT, NE, NE))
    arrays = dict(
        u=u, w_in=blocks(x["L0_attn_W_in"].T), b_in=x["L0_attn_b_in"].reshape(-1, P).T, w_x=blocks(w_x.T), b_x=b_x,
        w_dt=w_dt, b_dt=x["L0_attn_b_dt"].reshape(-1, P).T, a_log=a_log, d_skip=x["L0_attn_D"].reshape(-1, P).T,
        w_out=blocks(x["L0_attn_W_out"].T), b_out=b_out, w_ga=blocks(w_ga),
        b_g=_np.broadcast_to(x["L0_ffn_bg"], (P, TT, NE)), w_i=blocks(x["L0_ffn_Wi"].T), w_o=blocks(x["L0_ffn_Wo"].T),
        lora_b=lora, ident_in=_np.eye(P, dtype=f32), nsum_in=_np.tile(_np.eye(32, dtype=f32), (4, 1)), tri_in=tri)
    nc = _bacc.Bacc("TRN2", target_bir_lowering=False, num_devices=1, dynamic_dma_scratch_size=2048)
    ins, args = {}, {}
    for name, a in arrays.items():
        ins[f"in_{name}"] = _np.ascontiguousarray(a)
        args[name] = nc.dram_tensor(f"in_{name}", a.shape, _mybir.dt.from_np(a.dtype), kind="ExternalInput").ap()
    out = nc.dram_tensor("out_x", (NC, T, D), _mybir.dt.from_np(_np.dtype(f32)), kind="ExternalOutput").ap()
    block_program(nc, out=out, **args)
    r = _run(nc, [ins], core_ids=[0])
    got = r.results[0]["out_x"]
    return got.reshape(SEQ // T, BATCH, T, D).transpose(1, 0, 2, 3).reshape(BATCH, SEQ, D)
```

```python
from contextlib import ExitStack

import concourse.bass as bass
from concourse import mybir

F32 = mybir.dt.float32
F32R = mybir.dt.float32r
ALU = mybir.AluOpType
ACT = mybir.ActivationFunctionType
AX = mybir.AxisListType.X

P = 128
BATCH, SEQ, D = 4, 2048, 256
DI, NS, RANK = 512, 16, 16
FF, NE, LR = 1024, 4, 4
T = 512
NC = BATCH * SEQ // T
TT = T // P
KD = D // P
M = DI // P
J = P // 32
KG = NS // 4
STEPS = M * KG
UNITS = STEPS * J
NF = FF // P
NP = 2 * TT
EPS = 1e-5
BIG = 1e18

PE_SIDE = [
    "K1 late, S5 late, T4 late, J6 late | T5 late",
    " | J7 late",
    "S6 late, A0 pre, K2 late, A1 pre | S7 late",
    "E0 main | T6 late, B0 pre",
    "F0 post, F1 post | F2 post, B1 pre",
    "F3 post | ",
    "B2 pre, B3 pre | ",
    "C0 pre, T7 late | G0 post, E1 main",
    "G1 post | D0 pre, H0 post",
    "D1 pre | K3 late, E2 main, E3 main",
    "I0 post | J0 post",
    "J1 post, S0 post | T0 post, S1 post",
    "J2 post, T1 post | J3 post, S2 post, K0 post",
    "S3 post | ",
    "T2 post, J4 post, D2 pre, T3 post | ",
    "J5 post | D3 pre, S4 post",
]
ACT_SIDE = [
    "L1 main, S5 late |  | T4 late, R1 pre | ",
    "M1 main, J6 late |  | O0 pre, O1 pre, O2 pre | O3 pre, T5 late, S6 late",
    " |  | A0 pre, A1 pre | J7 late",
    " | S7 late | E0 main | ",
    "T6 late |  |  | ",
    "B0 pre |  | Z0 main | B1 pre",
    " |  |  | R2 post",
    "B2 pre, B3 pre | Q0 post, Q1 post | Q2 post, Q3 post | C0 pre, G0 post",
    " |  | G1 post, E1 main | D0 pre, T7 late",
    " |  | X0 post, D1 pre | L0 pre",
    "Z1 main |  | M0 pre | I0 post",
    "E2 main | J0 post | S0 post, J1 post | ",
    "S1 post |  |  | T0 post",
    "J2 post | T1 post, Z2 main, S2 post | J3 post | E3 main, S3 post",
    " |  | T2 post | D2 pre",
    " | Z3 main, J4 post | T3 post | S4 post, D3 pre, J5 post",
]
DVE_SIDE = [
    "N0 pre, N1 pre, K1 late, N2 pre |  |  | O0 pre, O1 pre, O2 pre, O3 pre, O4 pre",
    " |  | Y3 post | ",
    " |  |  | ",
    " |  |  | K2 late",
    "W0 main | F0 post |  | F1 post",
    "F2 post |  |  | F3 post",
    "P0 post, Y0 main | P1 post, P2 post | Q0 post, Q1 post | Q2 post, Q3 post, Q4 post",
    " |  |  | ",
    "C0 pre |  |  | W1 main",
    " | H0 post, H1 post, H2 post, R0 post, R1 post | R2 post, R3 post, R4 post, R5 post, M0 post, R6 post, R7 post | M1 post",
    "M2 post, Y1 main, M3 post | M4 post |  | ",
    " | K3 late |  | W2 main",
    " |  |  | ",
    " |  | K0 post | ",
    " | W3 main, Y2 main |  | ",
    " |  |  | ",
]
POOL_SIDE = [
    "S3 post, R4 late",
    "R5 late",
    "G3 post, V1 main, R6 late",
    "R7 late, U1 main",
    "",
    "",
    "S0 main",
    "G0 main",
    "",
    "S1 main",
    "V0 pre, G1 main",
    "U0 pre",
    "R0 post, S2 main",
    "",
    "R1 post, G2 main, R2 post, R3 post",
    "",
]
SP_SIDE = [
    "",
    "",
    "",
    "K1 late",
    "",
    "",
    "",
    "",
    "K2 late",
    "",
    "",
    "K3 late",
    "",
    "",
    "",
    "K0 post",
]
DECAYS = 3
BANKS = 4
BANK_JOBS = "ABCDEFGHIJTK"
PHASE = {"pre": 0, "main": 1, "post": 2, "late": 3}


def split_table(table):
    rows = [[[x.strip() for x in part.split(",") if x.strip()] for part in row.split("|")] for row in table]
    return [row + [[]] * (J - len(row)) for row in rows]


SIDE = {"pe": split_table(PE_SIDE), "act": split_table(ACT_SIDE), "dve": split_table(DVE_SIDE),
        "pool": split_table(POOL_SIDE), "sp": split_table(SP_SIDE)}


def bank_jobs():
    return [x for row in SIDE["pe"] for part in row for x in part if x[0] in BANK_JOBS]


def place(engine, letter, i):
    for s, row in enumerate(SIDE[engine]):
        for j, part in enumerate(row):
            for x in part:
                if x.startswith(f"{letter}{i}"):
                    return J * s + j + UNITS * PHASE[x.split()[1]]


def assign_banks():
    free = [0] * BANKS
    for _ in range(2):
        free, bank = [x - UNITS for x in free], {}
        for x in bank_jobs():
            bank[x] = free.index(min(free))
            letter, i = x[0], int(x[1])
            reader = {"F": "F", "K": "K", "H": "H"}.get(letter)
            at = place("dve", letter, i) if reader else place("act", "S" if letter == "J" else letter, i)
            free[bank[x]] = at - UNITS * PHASE[x.split()[1]]
    return bank


def parts_of(c):
    got = set()
    if 0 <= c < NC:
        got.add("main")
    if c + 1 < NC:
        got.add("pre")
    if 0 <= c - 1 < NC:
        got.add("post")
    if 0 <= c - 2 < NC:
        got.add("late")
    return got


BANK = assign_banks()


def used(job, c, off=0):
    def count(at):
        n = 0
        for body in range(-1, at + 1):
            for x in bank_jobs():
                if x.split()[1] in parts_of(body) and BANK[x] == BANK[job]:
                    n += 1
                if body == at and x == job:
                    break
        return n

    if isinstance(c, int):
        return count(c + off)
    first, slope = count(2 + off), count(3 + off) - count(2 + off)
    assert all(count(x + off) == first + (x - 2) * slope for x in range(2, NC - 2))
    return c * slope + (first - 2 * slope)


def block_program(nc, u, w_in, b_in, w_x, b_x, w_dt, b_dt, a_log, d_skip, w_out, b_out, w_ga, b_g, w_i, w_o,
                  lora_b, ident_in, nsum_in, tri_in, out):
    with ExitStack() as ctx:
        def sb(name, shape, dt=F32):
            return ctx.enter_context(nc.sbuf_tensor(name, shape, dt))

        def sem(name):
            return ctx.enter_context(nc.semaphore(name))

        bc_dram = nc.dram_tensor("bc_scratch", (2, NS, T), F32, kind="Internal").ap()
        rep_dram = nc.dram_tensor("rep_scratch", (2, M, P, T), F32, kind="Internal").ap()

        w_in_sb = sb("w_in_sb", [P, KD, 2 * DI])
        w_x_sb = sb("w_x_sb", [P, M, P])
        w_dt_st = sb("w_dt_st", [P, DI], F32R)
        w_out_sb = sb("w_out_sb", [P, M, D])
        w_ga_sb = sb("w_ga_sb", [P, KD, NE + NE * LR])
        w_i_sb = sb("w_i_sb", [P, KD, FF])
        w_o_sb = sb("w_o_sb", [P, NF, D])
        lora_st = sb("lora_st", [P, 2, FF], F32R)
        ident = sb("ident", [P, P])
        nsum = sb("nsum", [P, 32])
        tri = sb("tri", [P, TT, NE, NE])
        b_in_sb = sb("b_in_sb", [P, 2 * M])
        nb_z = sb("nb_z", [P, M])
        b_x_sb = sb("b_x_sb", [P, 1])
        b_dt_sb = sb("b_dt_sb", [P, M])
        d_sb = sb("d_sb", [P, M])
        a_sb = sb("a_sb", [P, UNITS])
        b_out_st = sb("b_out_st", [P, D], F32R)
        ones = sb("ones", [P, P], F32R)
        b_g_sb = sb("b_g_sb", [P, TT, NE])
        xin = sb("xin", [P, TT, D])
        xn_t = [sb(f"xn_t{i}", [P, KD, T]) for i in range(2)]
        x_t = [sb(f"x_t{i}", [P, M, T]) for i in range(2)]
        dbc = sb("dbc", [P, T])
        dt_st = sb("dt_st", [P, T], F32R)
        z_dt = sb("z_dt", [P, 2, T])
        e_dt = sb("e_dt", [P, 2, T])
        z_gate = [sb(f"z_gate{i}", [P, T]) for i in range(2)]
        e_gate = sb("e_gate", [P, T])
        gated = [sb(f"gated{i}", [P, M, T]) for i in range(2)]
        b_rep = sb("b_rep", [P, KG, T])
        c_rep = sb("c_rep", [P, KG, T])
        dt_rep = [sb(f"dt_rep{i}", [P, J, T]) for i in range(2)]
        dx_rep = [sb(f"dx_rep{i}", [P, J, T]) for i in range(2)]
        hs = [sb(f"hs{i}", [P, J, T]) for i in range(4)]
        state = [sb(f"state{i}", [P, UNITS]) for i in range(2)]
        state_next = [sb(f"state_next{i}", [P, UNITS]) for i in range(2)]
        xr = sb("xr", [P, TT, D])
        x1 = [sb(f"x1_{i}", [P, TT, D]) for i in range(2)]
        x2_t = sb("x2_t", [P, KD, T])
        low_t = sb("low_t", [P, T], F32R)
        r1 = [sb(f"r1_{i}", [P, T]) for i in range(2)]
        r2 = [sb(f"r2_{i}", [P, T]) for i in range(2)]
        r_t = sb("r_t", [P, NF, P])
        st1 = sb("st1", [P, TT, 6])
        mv1 = sb("mv1", [P, TT, 2])
        ve1 = sb("ve1", [P, TT])
        rs1 = sb("rs1", [P, TT])
        nt1 = sb("nt1", [P, TT])
        st2 = sb("st2", [P, TT, 6])
        mv2 = sb("mv2", [P, TT, 2])
        ve2 = sb("ve2", [P, TT])
        rs2 = sb("rs2", [P, TT])
        nt2 = sb("nt2", [P, TT])
        lg = sb("lg", [P, TT, NE])
        low = sb("low", [P, TT, NE * LR])
        mx = sb("mx", [P, TT])
        lm = sb("lm", [P, TT, NE])
        pexp = sb("pexp", [P, TT, NE])
        sm = sb("sm", [P, TT])
        rsm = sb("rsm", [P, TT])
        sc = sb("sc", [P, TT, NE])
        gt = sb("gt", [P, TT, NE, NE])
        eq = sb("eq", [P, TT, NE, NE])
        rank = sb("rank", [P, TT, NE])
        sel = sb("sel", [P, 2, TT, NE])
        change = sb("change", [P, TT, NE])
        wk = sb("wk", [P, 2, TT, NE])
        wgt = sb("wgt", [P, 2, TT])
        msk = sb("msk", [P, 2, TT, NE, LR])
        msk_hi = sb("msk_hi", [P, 2, TT, NE * LR], F32R)
        pk = sb("pk", [P, TT, 2, 2, 2, NE * LR])

        decay = [ctx.enter_context(nc.psum_tensor(f"decay{i}", [P, T], F32)) for i in range(DECAYS)]
        y_ps = ctx.enter_context(nc.psum_tensor("y_ps", [P, T], F32))
        banks = [ctx.enter_context(nc.psum_tensor(f"bank{i}", [P, 512], F32)) for i in range(BANKS)]
        filled = [sem(f"filled{i}") for i in range(BANKS)]
        freed = [sem(f"freed{i}") for i in range(BANKS)]

        (w_first, w_later, zeroed, a_ready, raw_rounded, weights_split, xin_loaded, ln1_part, ln1_root, ln1_newton, xn_ready,
         dt_hi, dt_lo, exp_dt, log_dt, delta_ready, dx_ready, bc_stored, rep_stored) = (sem(n) for n in (
            "w_first", "w_later", "zeroed", "a_ready", "raw_rounded", "weights_split", "xin_loaded", "ln1_part", "ln1_root",
            "ln1_newton", "xn_ready", "dt_hi", "dt_lo", "exp_dt", "log_dt", "delta_ready", "dx_ready",
            "bc_stored", "rep_stored"))
        rep_loaded = [sem(f"rep_loaded{i}") for i in range(2)]
        b_loaded = [sem(f"b_loaded{k}") for k in range(KG)]
        c_loaded = [sem(f"c_loaded{k}") for k in range(KG)]
        (decay_ready, input_ready, scan_done, state_moved, state_kept, prod_ready, nsum_done, y_read, gated_ready,
         clamp_z, log_z, sig_ready, silu_ready) = (sem(n) for n in (
            "decay_ready", "input_ready", "scan_done", "state_moved", "state_kept", "prod_ready", "nsum_done", "y_read",
            "gated_ready", "clamp_z", "log_z", "sig_ready", "silu_ready"))
        (xr_loaded, ln2_part, ln2_root, ln2_newton, x2_ready, router, router_exp, masks_ready, r1_ready,
         z2_ready) = (sem(n) for n in (
            "xr_loaded", "ln2_part", "ln2_root", "ln2_newton", "x2_ready", "router", "router_exp",
            "masks_ready", "r1_ready", "z2_ready"))
        sp_turn, last_sums = sem("sp_turn"), sem("last_sums")
        logits_ready, largest, compared = sem("logits_ready"), sem("largest"), sem("compared")
        mask_step, weight_step, weights_ready = sem("mask_step"), sem("weight_step"), sem("weights_ready")
        MASK_STEPS, WEIGHT_STEPS = 7, 4
        out_stored = [sem(f"out_stored{t}") for t in range(TT)]

        block = ctx.enter_context(nc.Block())

        def at_least(eng, s, value):
            if not (isinstance(value, int) and value <= 0):
                eng.wait_ge(s, value)

        def chunk_of(c, when):
            return c + {"pre": 1, "main": 0, "post": -1, "late": -2}[when]

        def is_last(q):
            return isinstance(q, int) and q == NC - 1

        def odd_of(par, when):
            return (par + {"pre": 1, "main": 0, "post": 1, "late": 0}[when]) % 2

        def wait_filled(eng, job, c):
            eng.wait_ge(filled[BANK[job]], used(job, c))
            return banks[BANK[job]], freed[BANK[job]]

        def wait_read(eng, c, when, letter, numbers, own=None):
            last = {}
            for place_, job in enumerate(bank_jobs()):
                if job[0] == letter and int(job[1]) in numbers:
                    off = PHASE[job.split()[1]] - PHASE[when]
                    last[BANK[job]] = max(last.get(BANK[job], (-9, 0, "")), (off, place_, job))
            for b, (off, _, job) in last.items():
                if b != own:
                    eng.wait_ge(freed[b], used(job, c, off))

        def sweep(eng, body):
            for c in (-1, 0, 1):
                body(c, c % 2, parts_of(c))
            with eng.Fori(1, (NC - 2) // 2) as pair:
                for odd in range(2):
                    body(pair * 2 + odd, odd, parts_of(2))
            for c in (NC - 2, NC - 1, NC, NC + 1):
                body(c, c % 2, parts_of(c))

        def side(engine, s, j, parts):
            for job in SIDE[engine][s][j]:
                if job.split()[1] in parts:
                    yield job[0], int(job[1]), job.split()[1], job

        raw_lora = hs[2][:].rearrange("p a t -> p (a t)").rearrange("p (a t) -> p a t", a=2)
        raw_b_out = hs[3][:, 0, 0:D]
        first_loads = ((w_in_sb[:], w_in), (ident[:], ident_in), (b_in_sb[:], b_in), (nb_z[:], b_in[:, M:2 * M]),
                       (w_x_sb[:], w_x), (b_x_sb[:], b_x), (hs[1][:, 0, :], w_dt), (b_dt_sb[:], b_dt),
                       (a_sb[:], a_log), (d_sb[:], d_skip), (nsum[:], nsum_in))
        later_loads = ((raw_lora, lora_b), (w_out_sb[:], w_out), (w_ga_sb[:], w_ga), (tri[:], tri_in),
                       (b_g_sb[:], b_g), (raw_b_out, b_out), (w_i_sb[:], w_i), (w_o_sb[:], w_o))

        def wait_first(eng):
            eng.wait_ge(w_first, 16 * len(first_loads))

        def wait_later(eng):
            eng.wait_ge(w_later, 16 * len(later_loads))

        @block.sync
        def _(sp):
            sp.dma_start(xin[:], u[0].rearrange("(t p) d -> p t d", p=P)).then_inc(xin_loaded, 16)
            for dst, src in first_loads:
                sp.dma_start(dst, src).then_inc(w_first, 16)
            for dst, src in later_loads:
                sp.dma_start(dst, src).then_inc(w_later, 16)

            def load_rep(c, m):
                for kind, dst in enumerate((dt_rep, dx_rep)):
                    for n in range(4):
                        sp.dma_start(dst[m % 2][32 * n:32 * n + 32, :, :],
                                     rep_dram[kind, m].rearrange("(j d) t -> d j t", j=J)).then_inc(rep_loaded[m % 2], 16)

            def load_bc(which, k):
                dst, s = ((b_rep, b_loaded), (c_rep, c_loaded))[which]
                for n in range(4):
                    sp.dma_start(dst[32 * n:32 * n + 32, k, :],
                                 bc_dram[which, 4 * k + n:4 * k + n + 1, :].to_broadcast([32, T])).then_inc(s[k], 16)

            def waits(*needs):
                for s_, at in needs:
                    at_least(sp, s_, at)
                    if not isinstance(at, int):
                        sp.sem_inc(sp_turn, 1)

            def filled_by(job, c):
                return filled[BANK[job]], used(job, c)

            def read_by(job, c):
                return freed[BANK[job]], used(job, c)

            def store_rep(c, pair):
                back = [(rep_loaded[i], 256 * c - (128 if pair == 0 else 0)) for i in range(2)]
                waits(*back, (delta_ready, 2 * c + pair + 1), (dx_ready, 2 * c + pair + 1))
                for kind, src in enumerate((e_dt, z_dt)):
                    sp.dma_start(rep_dram[kind, 2 * pair:2 * pair + 2].rearrange("m p t -> p m t"),
                                 src[:]).then_inc(rep_stored, 16)

            def chunk_rows(dram, c):
                return dram[bass.ds(c, 1)]

            def store_out(t, when, job, c, par):
                dst = chunk_rows(out, chunk_of(c, when))
                waits(read_by(job, c))
                sp.dma_start(dst[:, t * P:(t + 1) * P, :].rearrange("o p d -> p (o d)"),
                             x1[odd_of(par, when)][:, t, :]).then_inc(out_stored[t], 16)

            def body(c, par, parts):
                def past(m):
                    return (decay_ready, UNITS * c + KG * J * m), (input_ready, 2 * (STEPS * c + KG * m))

                for s in range(STEPS):
                    m, k = divmod(s, KG)
                    if "main" in parts and s == 0:
                        waits((prod_ready, STEPS * c))
                        load_bc(1, KG - 1)
                    if "main" in parts and k == 1 and m + 1 < M:
                        waits(*past(m), (rep_stored, 64 * c + 32 * (2 if m >= 1 else 1)))
                        load_rep(c, m + 1)
                    if "pre" in parts and s == 2 and (not isinstance(c, int) or c + 2 < NC):
                        src = chunk_rows(u, c + 2)
                        waits(filled_by("A1 pre", c))
                        sp.dma_start(xin[:], src.rearrange("o (t p) d -> p (o t) d", p=P)).then_inc(xin_loaded, 16)
                    if "main" in parts and s == 4:
                        store_rep(c, 1)
                    for _, t, when, job in side("sp", s, 0, parts):
                        store_out(t, when, job, c, par)
                    if "pre" in parts and s == 8:
                        back = [(x[kk], 64 * (c + 1)) for kk in range(KG) for x in (b_loaded, c_loaded)]
                        waits(read_by("C0 pre", c), *back)
                        sp.dma_start(bc_dram[0], dbc[16:32, :]).then_inc(bc_stored, 16)
                        sp.dma_start(bc_dram[1], dbc[48:64, :]).then_inc(bc_stored, 16)
                    if "main" in parts and s == 11:
                        src = chunk_rows(u, c)
                        if "post" in parts:
                            waits(filled_by("G1 post", c))
                        sp.dma_start(xr[:], src.rearrange("o (t p) d -> p (o t) d", p=P)).then_inc(xr_loaded, 16)
                    if "pre" in parts and s == 13:
                        store_rep(c + 1, 0)
                        waits((rep_stored, 64 * (c + 1) + 32), *past(M - 1))
                        load_rep(c + 1, 0)
                    if "pre" in parts and s >= 12:
                        if s == 12:
                            waits((bc_stored, 32 * (c + 2)))
                        waits((input_ready, 2 * (STEPS * c + s + 1)))
                        load_bc(0, s - 12)
                        if s > 12:
                            waits((prod_ready, STEPS * c + s))
                            load_bc(1, s - 13)

            sweep(sp, body)
            for t in range(TT):
                sp.wait_ge(out_stored[t], 16 * NC)

        @block.tensor
        def _(pe):
            wait_first(pe)

            def job_pe(letter, i, when, job, c, par):
                q, odd = chunk_of(c, when), odd_of(par, when)
                if letter == "S":
                    t, half = divmod(i, 2)
                    tile = next(x for x in bank_jobs() if x.startswith(f"J{i}"))
                    pe.wait_ge(r1_ready, NP * q + i + 1)
                    pe.matmul(banks[BANK[tile]][:], low_t[:, t * P:(t + 1) * P],
                              lora_st[:, 1, half * 512:(half + 1) * 512],
                              start=False, stop=True, skip_group_check=True).then_inc(z2_ready, 1)
                    return
                b = BANK[job]
                ps = banks[b]
                at_least(pe, freed[b], used(job, c) - 1)

                def needs(other, *numbers):
                    wait_read(pe, c, when, other, numbers, own=b)

                if letter in "AG":
                    pe.wait_ge(xn_ready if letter == "A" else x2_ready, TT * (q + 1))
                    src = xin if letter == "A" else xr
                    for t in range(TT):
                        mm = pe.transpose(ps[:, t * P:(t + 1) * P], src[:, t, i * P:(i + 1) * P], ident[:])
                elif letter in "BE":
                    if letter == "B":
                        needs("A", 0, 1)
                    col = i * P + (DI if letter == "E" else 0)
                    for k in range(KD):
                        mm = pe.matmul(ps[:], w_in_sb[:, k, col:col + P], xn_t[odd][:, k, :], start=k == 0, stop=k == KD - 1)
                elif letter == "C":
                    for k in range(M):
                        needs("B", k)
                        mm = pe.matmul(ps[:], w_x_sb[:, k, :], x_t[odd][:, k, :], start=k == 0, stop=k == M - 1)
                elif letter == "D":
                    if isinstance(c, int) and c < 0:
                        pe.wait_ge(weights_split, 1)
                    pe.wait_ge(dt_lo, q + 1)
                    mm = pe.matmul(ps[:], w_dt_st[:, i * P:(i + 1) * P], dt_st[:], start=True, stop=True)
                elif letter == "F":
                    pe.wait_ge(gated_ready, M * (q + 1))
                    for k in range(M):
                        pe.matmul(ps[:, 0:D], gated[odd][:, k, i * P:(i + 1) * P], w_out_sb[:, k, :], start=k == 0, stop=False)
                    mm = pe.matmul(ps[:, 0:D], ones[:], b_out_st[:], start=False, stop=True)
                elif letter == "H":
                    w = NE + NE * LR
                    needs("G", 0, 1)
                    for t in range(TT):
                        for k in range(KD):
                            mm = pe.matmul(ps[:, t * w:(t + 1) * w], x2_t[:, k, t * P:(t + 1) * P], w_ga_sb[:, k, :],
                                           start=k == 0, stop=k == KD - 1)
                elif letter == "I":
                    pe.wait_ge(masks_ready, q + 1)
                    for t in range(TT):
                        mm = pe.transpose(ps[:, t * P:(t + 1) * P], pk[:, t].rearrange("p a b c d -> p (a b c d)"), ident[:])
                elif letter == "J":
                    t, half = divmod(i, 2)
                    cols = slice(half * 512, (half + 1) * 512)
                    if i == 0:
                        needs("I", 0)
                    for k in range(KD):
                        pe.matmul(ps[:], x2_t[:, k, t * P:(t + 1) * P], w_i_sb[:, k, cols], start=k == 0, stop=False)
                    mm = pe.matmul(ps[:], low_t[:, t * P:(t + 1) * P], lora_st[:, 0, cols], start=False, stop=True)
                elif letter == "T":
                    if is_last(q):
                        pe.wait_ge(last_sums, i + 1)
                        for f in range(4):
                            mm = pe.transpose(ps[:, f * P:(f + 1) * P], r1[i % 2][:, f * P:(f + 1) * P], ident[:])
                    else:
                        wait_read(pe, c, when, "J", [i], own=b)
                        for f in range(4):
                            for r in (r1, r2):
                                mm = pe.matmul(ps[:, f * P:(f + 1) * P], r[i % 2][:, f * P:(f + 1) * P], ident[:],
                                               start=r is r1, stop=r is r2)
                elif letter == "K":
                    needs("T", 2 * i, 2 * i + 1)
                    for f in range(NF):
                        mm = pe.matmul(ps[:, 0:D], r_t[:, f, :], w_o_sb[:, f, :], start=f == 0, stop=f == NF - 1)
                mm.then_inc(filled[b], 1)

            def sum_states(c, s):
                m, k = divmod(s, KG)
                pe.wait_ge(prod_ready, STEPS * c + s + 1)
                if k == 0:
                    at_least(pe, y_read, M * c + m)
                for j in range(J):
                    mm = pe.matmul(y_ps[32 * j:32 * j + 32, :], nsum[:], hs[s % 4][:, j, :], start=k == 0,
                                   stop=k == KG - 1)
                mm.then_inc(nsum_done, 1)

            def body(c, par, parts):
                if isinstance(c, int) and c == 0:
                    wait_later(pe)
                    pe.wait_ge(weights_split, 3)
                for s in range(STEPS):
                    for job in side("pe", s, 0, parts):
                        job_pe(*job, c, par)
                    if s >= 2 and "main" in parts:
                        sum_states(c, s - 2)
                    if s < 2 and "post" in parts:
                        sum_states(c - 1, STEPS - 2 + s)
                    for job in side("pe", s, 1, parts):
                        job_pe(*job, c, par)

            sweep(pe, body)

        @block.scalar
        def _(act):
            nc.scalar.preload_act_table_set("natural_log_exp_and_others")
            wait_first(act)
            nc.scalar.activation(a_sb[:], a_sb[:], ACT.Exp).then_inc(a_ready, 1)
            act.wait_ge(a_ready, 1)
            nc.scalar.mul(a_sb[:], a_sb[:], -1.0).then_inc(a_ready, 1)
            nc.scalar.mul(nb_z[:], nb_z[:], -1.0).then_inc(a_ready, 1)
            act.wait_ge(a_ready, 3)

            def job_act(letter, i, when, job, c, par):
                q, odd = chunk_of(c, when), odd_of(par, when)
                big = not isinstance(q, int)
                if letter == "A":
                    ps, free = wait_filled(act, job, c)
                    nc.scalar.copy(xn_t[odd][:, i, :], ps[:]).then_inc(free, 1)
                elif letter == "B":
                    at_least(act, y_read, M * (q - 2) + i + 1 if big or q >= 2 else 0)
                    at_least(act, dx_ready, 2 * (q - 1) if big or q >= 2 else 0)
                    ps, free = wait_filled(act, job, c)
                    nc.scalar.activation(x_t[odd][:, i, :], ps[:], ACT.Identity, bias=b_in_sb[:, i:i + 1]).then_inc(free, 1)
                elif letter == "C":
                    at_least(act, bc_stored, 32 * q)
                    at_least(act, dt_lo, q)
                    ps, free = wait_filled(act, job, c)
                    nc.scalar.activation(dbc[:], ps[:], ACT.Identity, bias=b_x_sb[:, 0:1]).then_inc(free, 1)
                    wait_read(act, c, when, "C", [0])
                    nc.scalar.activation(dt_st[:], dbc[:], ACT.Identity).then_inc(dt_hi, 1)
                elif letter == "D":
                    if i % 2 == 0:
                        at_least(act, rep_stored, 64 * q + 32 * (i // 2))
                    ps, free = wait_filled(act, job, c)
                    nc.scalar.activation(z_dt[:, i % 2, :], ps[:], ACT.Relu, bias=b_dt_sb[:, i:i + 1])
                    nc.scalar.activation(e_dt[:, i % 2, :], ps[:], ACT.Abs, bias=b_dt_sb[:, i:i + 1]).then_inc(free, 1)
                elif letter == "L":
                    wait_read(act, c, when, "D", (2 * i, 2 * i + 1))
                    nc.scalar.activation(e_dt[:], e_dt[:], ACT.Exp, scale=-1.0).then_inc(exp_dt, 1)
                elif letter == "M":
                    act.wait_ge(exp_dt, 2 * q + i + 1)
                    nc.scalar.activation(e_dt[:], e_dt[:], ACT.Ln, bias=1.0).then_inc(log_dt, 1)
                elif letter == "E":
                    at_least(act, gated_ready, M * q + i - 1)
                    ps, free = wait_filled(act, job, c)
                    nc.scalar.activation(z_gate[i % 2][:], ps[:], ACT.Identity, bias=b_in_sb[:, M + i:M + i + 1])
                    at_least(act, silu_ready, M * q + i)
                    nc.scalar.activation(e_gate[:], ps[:], ACT.Exp, scale=-1.0, bias=nb_z[:, i:i + 1]).then_inc(free, 1)
                elif letter == "Z":
                    act.wait_ge(clamp_z, M * q + i + 1)
                    nc.scalar.activation(e_gate[:], e_gate[:], ACT.Ln).then_inc(log_z, 1)
                    act.wait_ge(log_z, M * q + i + 1)
                    nc.scalar.activation(e_gate[:], e_gate[:], ACT.Exp, scale=-1.0).then_inc(sig_ready, 1)
                elif letter == "R":
                    ve, rs, part, root = (ve1, rs1, ln1_part, ln1_root) if i == 1 else (ve2, rs2, ln2_part, ln2_root)
                    act.wait_ge(part, 3 * (q + 1))
                    nc.scalar.activation(rs[:], ve[:], ACT.Ln).then_inc(root, 1)
                    act.wait_ge(root, 2 * q + 1)
                    nc.scalar.activation(rs[:], rs[:], ACT.Exp, scale=-0.5).then_inc(root, 1)
                elif letter in "OQ":
                    src, dst, rs, nt, newton, done = ((xin, xin, rs1, nt1, ln1_newton, xn_ready) if letter == "O"
                                                      else (x1[odd], xr, rs2, nt2, ln2_newton, x2_ready))
                    act.wait_ge(newton, 5 * (q + 1))
                    nc.scalar.activation(dst[:, i, :], src[:, i, :], ACT.Identity, scale=rs[:, i:i + 1],
                                         bias=nt[:, i:i + 1]).then_inc(done, 1)
                elif letter == "G":
                    ps, free = wait_filled(act, job, c)
                    nc.scalar.copy(x2_t[:, i, :], ps[:]).then_inc(free, 1)
                elif letter == "X":
                    act.wait_ge(router, q + 1)
                    nc.scalar.activation(pexp[:], lm[:], ACT.Exp).then_inc(router_exp, 1)
                elif letter == "I":
                    ps, free = wait_filled(act, job, c)
                    nc.scalar.activation(low_t[:], ps[:], ACT.Identity).then_inc(free, 1)
                elif letter == "J":
                    if i == 0:
                        act.wait_ge(weights_ready, q + 1)
                    before = next(x for x in bank_jobs() if x.startswith(f"T{(i - 2) % NP}"))
                    if i >= 2 or not isinstance(q, int) or q >= 1:
                        off = PHASE[before.split()[1]] - PHASE[when] - (i < 2)
                        if BANK[before] != BANK[job]:
                            act.wait_ge(filled[BANK[before]], used(before, c, off))
                    ps, _ = wait_filled(act, job, c)
                    nc.scalar.activation(r1[i % 2][:], ps[:], ACT.Relu, scale=wgt[:, 0, i // 2:i // 2 + 1]).then_inc(r1_ready, 1)
                elif letter == "S":
                    act.wait_ge(z2_ready, NP * q + i + 1)
                    b = BANK[next(x for x in bank_jobs() if x.startswith(f"J{i}"))]
                    nc.scalar.activation(r2[i % 2][:], banks[b][:], ACT.Relu,
                                         scale=wgt[:, 1, i // 2:i // 2 + 1]).then_inc(freed[b], 1)
                elif letter == "T":
                    ps, free = wait_filled(act, job, c)
                    nc.scalar.copy(r_t[:, 4 * (i % 2):4 * (i % 2) + 4, :].rearrange("p f t -> p (f t)"), ps[:]).then_inc(free, 1)

            def body(c, par, parts):
                for s in range(STEPS):
                    m, k = divmod(s, KG)
                    for j in range(J):
                        if "main" in parts:
                            n = UNITS * c + J * s + j
                            if j == 0 and k == 0:
                                act.wait_ge(rep_loaded[m % 2], 256 * c + 128 * (m // 2 + 1))
                            at_least(act, scan_done, n if s == j == 0 else n - DECAYS + 1)
                            nc.scalar.activation(decay[(J * s + j) % DECAYS][:], dt_rep[m % 2][:, j, :], ACT.Exp,
                                                 scale=a_sb[:, J * s + j:J * s + j + 1]).then_inc(decay_ready, 1)
                        if j in (1, 2) and s >= 1 and "main" in parts:
                            (move_state, keep_state)[j - 1](c, par, s - 1)
                        if j in (1, 2) and s == 0 and "post" in parts:
                            (move_state, keep_state)[j - 1](c - 1, 1 - par, STEPS - 1)
                        for job in side("act", s, j, parts):
                            job_act(*job, c, par)

            def move_state(c, par, s):
                cols = slice(J * s, J * s + J)
                act.wait_ge(scan_done, UNITS * c + J * (s + 1))
                nc.scalar.copy(state[par][:, cols], state_next[par][:, cols]).then_inc(state_moved, 1)

            def keep_state(c, par, s):
                act.wait_ge(state_moved, STEPS * c + s + 1)
                nc.scalar.copy(state_next[par][:, J * s:J * s + J], hs[s % 4][:, :, T - 1]).then_inc(state_kept, 1)

            sweep(act, body)

        @block.vector
        def _(dve):
            v = nc.vector
            for par in range(2):
                v.memset(state[par][:], 0.0)
                v.memset(state_next[par][:], 0.0).then_inc(zeroed, 1)
            def split_weights(st, raw, done):
                v.tensor_copy(st[:], raw).then_inc(raw_rounded, 1)
                dve.wait_ge(raw_rounded, done)
                for lo in (32, 96):
                    last = v.tensor_tensor(st[lo:lo + 32], raw[lo:lo + 32], st[lo:lo + 32].bitcast(F32), ALU.subtract)
                last.then_inc(weights_split, 1)

            def stats(i, q, src, st, mv, ve, part):
                at_least(dve, part, 3 * q + i if i > 0 else 0)
                if i == 0:
                    for t in range(TT):
                        last = v.bn_stats(st[:, t, :], src[:, t, :])
                elif i == 1:
                    v.memset(ve[:], EPS)
                    for t in range(TT):
                        last = v.bn_aggr(mv[:, t, :], st[:, t, :])
                else:
                    last = v.tensor_tensor(ve[:], mv[:, :, 1], ve[:], ALU.add)
                last.then_inc(part, 1)

            def deviations(i, q, mv, ve, rs, nt, root, newton):
                if i == 0:
                    dve.wait_ge(root, 2 * (q + 1))
                    last = v.tensor_tensor(nt[:], rs[:], rs[:], ALU.mult)
                else:
                    dve.wait_ge(newton, 5 * q + i)
                if i == 1:
                    last = v.tensor_tensor(nt[:], nt[:], ve[:], ALU.mult)
                elif i == 2:
                    last = v.tensor_scalar(nt[:], nt[:], -0.5, 1.5, ALU.mult, ALU.add)
                elif i == 3:
                    last = v.tensor_tensor(rs[:], rs[:], nt[:], ALU.mult)
                elif i == 4:
                    last = v.scalar_tensor_tensor(out=nt[:], in0=mv[:, :, 0], scalar=-1.0, in1=rs[:], op0=ALU.mult,
                                                  op1=ALU.mult)
                last.then_inc(newton, 1)

            def job_dve(letter, i, when, job, c, par):
                q, odd = chunk_of(c, when), odd_of(par, when)
                if letter == "N":
                    if i == 0:
                        dve.wait_ge(xin_loaded, 16 * (q + 1))
                    stats(i, q, xin, st1, mv1, ve1, ln1_part)
                elif letter == "O":
                    deviations(i, q, mv1, ve1, rs1, nt1, ln1_root, ln1_newton)
                elif letter == "P":
                    if i == 0:
                        wait_read(dve, c, when, "F", range(TT))
                    stats(i, q, x1[odd], st2, mv2, ve2, ln2_part)
                elif letter == "Q":
                    deviations(i, q, mv2, ve2, rs2, nt2, ln2_root, ln2_newton)
                elif letter == "C":
                    dve.wait_ge(dt_hi, q + 1)
                    v.tensor_tensor(dt_st[64:128], dbc[64:128], dt_st[64:128].bitcast(F32), ALU.subtract).then_inc(dt_lo, 1)
                elif letter == "W":
                    wait_read(dve, c, when, "E", [i])
                    v.tensor_scalar(e_gate[:], e_gate[:], BIG, 1.0, ALU.min, ALU.add).then_inc(clamp_z, 1)
                elif letter == "Y":
                    dve.wait_ge(nsum_done, STEPS * q + KG * (i + 1))
                    v.scalar_tensor_tensor(out=gated[odd][:, i, :], in0=x_t[odd][:, i, :], scalar=d_sb[:, i:i + 1],
                                           in1=y_ps[:], op0=ALU.mult, op1=ALU.add).then_inc(y_read, 1)
                elif letter == "F":
                    if i == 0:
                        dve.wait_ge(xr_loaded, 16 * (q + 1))
                    at_least(dve, out_stored[i], 16 * (q - 1))
                    ps, free = wait_filled(dve, job, c)
                    v.tensor_tensor(x1[odd][:, i, :], ps[:, 0:D], xr[:, i, :], ALU.add).then_inc(free, 1)
                elif letter == "K":
                    ps, free = wait_filled(dve, job, c)
                    v.tensor_tensor(x1[odd][:, i, :], ps[:, 0:D], x1[odd][:, i, :], ALU.add).then_inc(free, 1)
                elif letter == "H" and i == 0:
                    ps, free = wait_filled(dve, job, c)
                    z = ps[:, 0:TT * (NE + NE * LR)].rearrange("p (t w) -> p t w", t=TT)
                    v.tensor_tensor(lg[:], z[:, :, 0:NE], b_g_sb[:], ALU.add).then_inc(logits_ready, 1)
                    v.tensor_copy(low[:], z[:, :, NE:]).then_inc(free, 1)
                elif letter == "H" and i == 1:
                    dve.wait_ge(logits_ready, q + 1)
                    v.tensor_reduce(mx[:], lg[:], AX, ALU.max).then_inc(largest, 1)
                    other = lg[:].unsqueeze(2).to_broadcast([P, TT, NE, NE])
                    own = lg[:].unsqueeze(3).to_broadcast([P, TT, NE, NE])
                    v.tensor_tensor(gt[:], other, own, ALU.is_gt)
                    v.tensor_tensor(eq[:], other, own, ALU.is_equal).then_inc(compared, 1)
                elif letter == "H":
                    dve.wait_ge(largest, q + 1)
                    v.tensor_tensor(lm[:], lg[:], mx[:].unsqueeze(2).to_broadcast([P, TT, NE]), ALU.subtract).then_inc(router, 1)
                elif letter == "R":
                    mask_factors(i, q)
                elif letter == "M":
                    weigh_choices(i, q)

            def mask_factors(i, q):
                flat = msk[:].rearrange("p a t e r -> p a t (e r)")
                if i == 0:
                    dve.wait_ge(compared, q + 1)
                    last = v.tensor_tensor(eq[:], eq[:], tri[:], ALU.mult)
                else:
                    dve.wait_ge(mask_step, MASK_STEPS * q + i)
                if i == 1:
                    last = v.tensor_tensor(gt[:], gt[:], eq[:], ALU.add)
                elif i == 2:
                    last = v.tensor_reduce(rank[:], gt[:], AX, ALU.add)
                elif i == 3:
                    for a in range(2):
                        last = v.tensor_scalar(sel[:, a], rank[:], float(a), None, ALU.is_equal)
                elif i == 4:
                    last = v.tensor_tensor(change[:], sel[:, 1], sel[:, 0], ALU.subtract)
                elif i == 5:
                    lw = low[:].rearrange("p t (e r) -> p t e r", e=NE)
                    for a, mask in enumerate((sel[:, 0], change[:])):
                        last = v.tensor_tensor(msk[:, a], lw, mask.unsqueeze(3).to_broadcast([P, TT, NE, LR]), ALU.mult)
                elif i == 6:
                    last = v.tensor_copy(msk_hi[:], flat)
                elif i == 7:
                    hi = msk_hi[:].bitcast(F32)
                    for a in range(2):
                        both = [P, TT, 2, NE * LR]
                        v.tensor_copy(pk[:, :, a, :, 0], hi[:, a].unsqueeze(2).to_broadcast(both))
                        last = v.tensor_tensor(pk[:, :, a, :, 1], flat[:, a].unsqueeze(2).to_broadcast(both),
                                               hi[:, a].unsqueeze(2).to_broadcast(both), ALU.subtract)
                last.then_inc(masks_ready if i == MASK_STEPS else mask_step, 1)

            def weigh_choices(i, q):
                if i == 0:
                    dve.wait_ge(router_exp, q + 1)
                    last = v.tensor_reduce(sm[:], pexp[:], AX, ALU.add)
                else:
                    dve.wait_ge(weight_step, WEIGHT_STEPS * q + i)
                if i == 1:
                    last = v.reciprocal(rsm[:], sm[:])
                elif i == 2:
                    last = v.tensor_tensor(sc[:], pexp[:], rsm[:].unsqueeze(2).to_broadcast([P, TT, NE]), ALU.mult)
                elif i == 3:
                    dve.wait_ge(mask_step, MASK_STEPS * q + 4)
                    for a in range(2):
                        last = v.tensor_tensor(wk[:, a], sel[:, a], sc[:], ALU.mult)
                elif i == 4:
                    last = v.tensor_reduce(wgt[:], wk[:], AX, ALU.add)
                last.then_inc(weights_ready if i == WEIGHT_STEPS else weight_step, 1)

            def scan_input(c, par, s, half):
                m, k = divmod(s, KG)
                if half == 0:
                    if k == 0:
                        dve.wait_ge(rep_loaded[m % 2], 256 * c + 128 * (m // 2 + 1))
                    if m == 0:
                        dve.wait_ge(b_loaded[k], 64 * (c + 1))
                    at_least(dve, nsum_done, STEPS * c + s - 3)
                js = slice(2 * half, 2 * half + 2)
                v.tensor_tensor(hs[s % 4][:, js, :], dx_rep[m % 2][:, js, :],
                                b_rep[:, k, :].unsqueeze(1).to_broadcast([P, 2, T]), ALU.mult).then_inc(input_ready, 1)

            def body(c, par, parts):
                for s in range(STEPS):
                    if "main" not in parts and "pre" in parts and s == 2:
                        wait_first(dve)
                        split_weights(w_dt_st, hs[1][:, 0, :], 1)
                    for j in range(J):
                        if "main" in parts and j % 2 == 0:
                            if s + 1 < STEPS:
                                scan_input(c, par, s + 1, j // 2)
                            elif "pre" in parts:
                                scan_input(c + 1, 1 - par, 0, j // 2)
                            dve.wait_ge(input_ready, 2 * (STEPS * c + s) + j // 2 + 1)
                        if "main" in parts:
                            dve.wait_ge(decay_ready, UNITS * c + J * s + j + 1)
                            h = hs[s % 4][:, j, :]
                            v.tensor_tensor_scan(h, decay[(J * s + j) % DECAYS][:], h, state[par][:, J * s + j:J * s + j + 1],
                                                 ALU.mult, ALU.add).then_inc(scan_done, 1)
                        for job in side("dve", s, j, parts):
                            job_dve(*job, c, par)
                if "main" not in parts and "pre" in parts:
                    wait_later(dve)
                    v.tensor_scalar(ones[:], ident[:], 0.0, 1.0, ALU.mult, ALU.add)
                    split_weights(lora_st, raw_lora, 2)
                    split_weights(b_out_st, raw_b_out, 3)
                    dve.wait_ge(weights_split, 3)
                    for half in range(2):
                        scan_input(0, 0, 0, half)

            sweep(dve, body)

        @block.gpsimd
        def _(pool):
            wait_later(pool)

            def job_pool(letter, i, when, job, c, par):
                q, odd = chunk_of(c, when), odd_of(par, when)
                g = nc.gpsimd
                if letter == "U":
                    pool.wait_ge(delta_ready, 2 * q + i + 1)
                    g.tensor_tensor(z_dt[:], e_dt[:], x_t[odd][:, 2 * i:2 * i + 2, :], ALU.mult).then_inc(dx_ready, 1)
                elif letter == "S":
                    pool.wait_ge(sig_ready, M * q + i + 1)
                    g.tensor_tensor(z_gate[i % 2][:], z_gate[i % 2][:], e_gate[:], ALU.mult).then_inc(silu_ready, 1)
                elif letter == "G":
                    pool.wait_ge(y_read, M * q + i + 1)
                    pool.wait_ge(silu_ready, M * q + i + 1)
                    g.tensor_tensor(gated[odd][:, i, :], gated[odd][:, i, :], z_gate[i % 2][:], ALU.mult).then_inc(gated_ready, 1)
                elif letter == "R" and is_last(q):
                    wait_read(pool, c, when, "J", [i])
                    g.tensor_tensor(r1[i % 2][:], r1[i % 2][:], r2[i % 2][:], ALU.add).then_inc(last_sums, 1)
                elif letter == "V":
                    pool.wait_ge(log_dt, 2 * q + i + 1)
                    g.tensor_tensor(e_dt[:], e_dt[:], z_dt[:], ALU.add).then_inc(delta_ready, 1)

            def times_c(c, s):
                k = s % KG
                pool.wait_ge(scan_done, UNITS * c + J * (s + 1))
                pool.wait_ge(state_kept, STEPS * c + s + 1)
                if s < KG:
                    pool.wait_ge(c_loaded[k], 64 * (c + 1))
                nc.gpsimd.tensor_tensor(hs[s % 4][:], hs[s % 4][:], c_rep[:, k, :].unsqueeze(1).to_broadcast([P, J, T]),
                                        ALU.mult).then_inc(prod_ready, 1)

            def body(c, par, parts):
                for s in range(STEPS):
                    if s >= 1 and "main" in parts:
                        times_c(c, s - 1)
                    if s == 0 and "post" in parts:
                        times_c(c - 1, STEPS - 1)
                    for job in side("pool", s, 0, parts):
                        job_pool(*job, c, par)

            sweep(pool, body)


def kernel(**inputs):
    import numpy as _np
    import concourse.bacc as _bacc
    from concourse import mybir as _mybir
    from concourse.bass_utils import run_bass_kernel_spmd as _run

    x = {k: _np.asarray(a) for k, a in inputs.items()}
    f32 = _np.float32

    def blocks(a):
        return a.reshape(-1, P, a.shape[-1]).transpose(1, 0, 2)

    u = x["L0_attn_u"].reshape(BATCH, SEQ // T, T, D).transpose(1, 0, 2, 3).reshape(NC, T, D)
    wx, bx = x["L0_attn_W_x"], x["L0_attn_b_x"]
    w_x, b_x = _np.zeros((P, DI), f32), _np.zeros((P, 1), f32)
    for at, frm in ((0, 0), (16, RANK), (32, 0), (48, RANK + NS), (64, 0), (96, 0)):
        w_x[at:at + 16], b_x[at:at + 16, 0] = wx[frm:frm + 16], bx[frm:frm + 16]
    w_dt = _np.zeros((P, DI), f32)
    for at in (0, 32, 64, 96):
        w_dt[at:at + RANK] = x["L0_attn_W_dt"].T
    b_out = _np.zeros((P, D), f32)
    b_out[0] = b_out[32] = x["L0_attn_b_out"]
    bcat = x["L0_ffn_B"].transpose(0, 2, 1).reshape(NE * LR, FF)
    lora = _np.zeros((P, 2, FF), f32)
    for choice in range(2):
        for at in range(0, 64, 16):
            lora[64 * choice + at:64 * choice + at + 16, choice] = bcat
    w_ga = _np.concatenate([x["L0_ffn_Wg"], x["L0_ffn_A"].reshape(NE * LR, D)], 0).T
    a_log = x["L0_attn_A_log"].reshape(M, J, 32, KG, 4).transpose(4, 2, 0, 3, 1).reshape(P, UNITS)
    tri = _np.broadcast_to(_np.tril(_np.ones((NE, NE), f32), -1), (P, TT, NE, NE))
    arrays = dict(
        u=u, w_in=blocks(x["L0_attn_W_in"].T), b_in=x["L0_attn_b_in"].reshape(-1, P).T, w_x=blocks(w_x.T), b_x=b_x,
        w_dt=w_dt, b_dt=x["L0_attn_b_dt"].reshape(-1, P).T, a_log=a_log, d_skip=x["L0_attn_D"].reshape(-1, P).T,
        w_out=blocks(x["L0_attn_W_out"].T), b_out=b_out, w_ga=blocks(w_ga),
        b_g=_np.broadcast_to(x["L0_ffn_bg"], (P, TT, NE)), w_i=blocks(x["L0_ffn_Wi"].T), w_o=blocks(x["L0_ffn_Wo"].T),
        lora_b=lora, ident_in=_np.eye(P, dtype=f32), nsum_in=_np.tile(_np.eye(32, dtype=f32), (4, 1)), tri_in=tri)
    nc = _bacc.Bacc("TRN2", target_bir_lowering=False, num_devices=1, dynamic_dma_scratch_size=2048)
    ins, args = {}, {}
    for name, a in arrays.items():
        ins[f"in_{name}"] = _np.ascontiguousarray(a)
        args[name] = nc.dram_tensor(f"in_{name}", a.shape, _mybir.dt.from_np(a.dtype), kind="ExternalInput").ap()
    out = nc.dram_tensor("out_x", (NC, T, D), _mybir.dt.from_np(_np.dtype(f32)), kind="ExternalOutput").ap()
    block_program(nc, out=out, **args)
    r = _run(nc, [ins], core_ids=[0])
    got = r.results[0]["out_x"]
    return got.reshape(SEQ // T, BATCH, T, D).transpose(1, 0, 2, 3).reshape(BATCH, SEQ, D)
```
